# Optimizing a Trainium2 kernel written in Bass

```python
import numpy as np
import jax
import jax.numpy as jnp

def _softmax(x, axis=-1):
    return jax.nn.softmax(x, axis=axis)

def _gelu(x):
    return jax.nn.gelu(x, approximate=True)

def _silu(x):
    return jax.nn.silu(x)

def _sigmoid(x):
    return jax.nn.sigmoid(x)

def _layernorm(x, axis=-1, eps=1e-05):
    m = jnp.mean(x, axis=axis, keepdims=True)
    v = jnp.var(x, axis=axis, keepdims=True)
    return (x - m) / jnp.sqrt(v + eps)

def _scatter_add(tgt, idx, src, axis=0):
    return tgt.at[idx].add(src)

def _segment_sum(src, seg, n):
    return jax.ops.segment_sum(src, seg, n)
kernel_name = 'mk_audio_tower_d1_tok_audfeat1024_r4_93ba7c'

def setup_inputs(seed: int=0):
    np.random.seed(seed)
    _w = jnp.asarray

    def _rec_inputs():
        import jax
        import jax.numpy as jnp
        _rk = jax.random.key(seed)
        x = -0.000125008 + 0.999885 * jax.random.normal(jax.random.fold_in(_rk, 1), (32, 375, 256), jnp.float32)
        return x
    x = _rec_inputs()

    def _L0_tok_setup():
        import jax, jax.numpy as jnp
        import numpy as np
        D_MODEL = 256
        STRIDE = 2
        KERNEL = 2
        INIT_STD = 0.02
        EPS = 1e-05
        key = jax.random.key(seed)
        k1, k2 = jax.random.split(key)
        hidden_states = jax.random.normal(k1, (4, 2048, D_MODEL), dtype=jnp.float32)
        conv_w = INIT_STD * jax.random.normal(k2, (D_MODEL, D_MODEL, KERNEL), dtype=jnp.float32)
        conv_b = jnp.zeros((D_MODEL,), dtype=jnp.float32)
        ln_gamma = jnp.ones((D_MODEL,), dtype=jnp.float32)
        ln_beta = jnp.zeros((D_MODEL,), dtype=jnp.float32)
        return {'hidden_states': hidden_states, 'conv_w': conv_w, 'conv_b': conv_b, 'ln_gamma': ln_gamma, 'ln_beta': ln_beta}
    _L0_tok_all = _L0_tok_setup()
    _L0_tok_in = {k: v for k, v in _L0_tok_all.items() if k in ('conv_w', 'conv_b', 'ln_gamma', 'ln_beta')}
    del _L0_tok_all

    def _L0_attn_setup():
        import jax, jax.numpy as jnp
        import numpy as np
        import math
        B, S, D = (4, 512, 256)
        H = 16
        HD = D // H
        DL = 64
        LAMBDA_DECAY = 0.01
        key = jax.random.key(seed)
        ks = jax.random.split(key, 8)
        sc = lambda fan_in: 1.0 / math.sqrt(fan_in)
        return {'x': jax.random.normal(ks[0], (B, S, D), dtype=jnp.float32), 'W_q': jax.random.normal(ks[1], (D, D), dtype=jnp.float32) * sc(D), 'W_k': jax.random.normal(ks[2], (D, D), dtype=jnp.float32) * sc(D), 'W_v': jax.random.normal(ks[3], (D, D), dtype=jnp.float32) * sc(D), 'W_o': jax.random.normal(ks[4], (D, D), dtype=jnp.float32) * sc(D), 'W_down_kv': jax.random.normal(ks[5], (D, DL), dtype=jnp.float32) * sc(D), 'W_up_k': jax.random.normal(ks[6], (DL, D), dtype=jnp.float32) * sc(DL), 'W_up_v': jax.random.normal(ks[7], (DL, D), dtype=jnp.float32) * sc(DL)}
    _L0_attn_all = _L0_attn_setup()
    _L0_attn_in = {k: v for k, v in _L0_attn_all.items() if k in ('W_q', 'W_k', 'W_v', 'W_o', 'W_down_kv', 'W_up_k', 'W_up_v')}
    del _L0_attn_all

    def _L0_ffn_setup():
        import jax, jax.numpy as jnp
        import numpy as np
        E = 16
        F_C = 2.0
        D = 256
        I = 4 * D
        IS = 2 * D
        B, S = (4, 256)
        key = jax.random.key(seed)
        ks = jax.random.split(key, 8)
        w = 0.02
        return {'hidden_states': jax.random.normal(ks[0], (B, S, D), dtype=jnp.float32), 'gate_w': jax.random.normal(ks[1], (E, D), dtype=jnp.float32) * w, 'Wg': jax.random.normal(ks[2], (E, I, D), dtype=jnp.float32) * w, 'Wu': jax.random.normal(ks[3], (E, I, D), dtype=jnp.float32) * w, 'Wd': jax.random.normal(ks[4], (E, D, I), dtype=jnp.float32) * w, 'Sg': jax.random.normal(ks[5], (IS, D), dtype=jnp.float32) * w, 'Su': jax.random.normal(ks[6], (IS, D), dtype=jnp.float32) * w, 'Sd': jax.random.normal(ks[7], (D, IS), dtype=jnp.float32) * w}
    _L0_ffn_all = _L0_ffn_setup()
    _L0_ffn_in = {k: v for k, v in _L0_ffn_all.items() if k in ('gate_w', 'Wg', 'Wu', 'Wd', 'Sg', 'Su', 'Sd')}
    del _L0_ffn_all
    return {'x': x, 'L0_tok_conv_w': _L0_tok_in['conv_w'], 'L0_tok_conv_b': _L0_tok_in['conv_b'], 'L0_tok_ln_gamma': _L0_tok_in['ln_gamma'], 'L0_tok_ln_beta': _L0_tok_in['ln_beta'], 'L0_attn_W_q': _L0_attn_in['W_q'], 'L0_attn_W_k': _L0_attn_in['W_k'], 'L0_attn_W_v': _L0_attn_in['W_v'], 'L0_attn_W_o': _L0_attn_in['W_o'], 'L0_attn_W_down_kv': _L0_attn_in['W_down_kv'], 'L0_attn_W_up_k': _L0_attn_in['W_up_k'], 'L0_attn_W_up_v': _L0_attn_in['W_up_v'], 'L0_ffn_gate_w': _L0_ffn_in['gate_w'], 'L0_ffn_Wg': _L0_ffn_in['Wg'], 'L0_ffn_Wu': _L0_ffn_in['Wu'], 'L0_ffn_Wd': _L0_ffn_in['Wd'], 'L0_ffn_Sg': _L0_ffn_in['Sg'], 'L0_ffn_Su': _L0_ffn_in['Su'], 'L0_ffn_Sd': _L0_ffn_in['Sd']}

def reference(x, L0_tok_conv_w, L0_tok_conv_b, L0_tok_ln_gamma, L0_tok_ln_beta, L0_attn_W_q, L0_attn_W_k, L0_attn_W_v, L0_attn_W_o, L0_attn_W_down_kv, L0_attn_W_up_k, L0_attn_W_up_v, L0_ffn_gate_w, L0_ffn_Wg, L0_ffn_Wu, L0_ffn_Wd, L0_ffn_Sg, L0_ffn_Su, L0_ffn_Sd):
    import jax
    import jax.numpy as jnp

    def _L0_tok_ref(hidden_states, conv_w, conv_b, ln_gamma, ln_beta):
        import jax, jax.numpy as jnp
        import numpy as np
        D_MODEL = 256
        STRIDE = 2
        KERNEL = 2
        INIT_STD = 0.02
        EPS = 1e-05
        B, L, D = hidden_states.shape
        pad_len = -L % STRIDE
        if pad_len:
            hidden_states = jnp.pad(hidden_states, ((0, 0), (0, pad_len), (0, 0)))
            L = L + pad_len
        xb = hidden_states.reshape(B, L // STRIDE, STRIDE, D)
        x = jnp.einsum('btki,oik->bto', xb, conv_w) + conv_b
        x = x + xb.mean(axis=2)
        mu = x.mean(axis=-1, keepdims=True)
        var = jnp.mean(jnp.square(x - mu), axis=-1, keepdims=True)
        x = (x - mu) * jax.lax.rsqrt(var + EPS) * ln_gamma + ln_beta
        return x

    def _L0_attn_ref(x, W_q, W_k, W_v, W_o, W_down_kv, W_up_k, W_up_v):
        import jax, jax.numpy as jnp
        import numpy as np
        import math
        B, S, D = (4, 512, 256)
        H = 16
        HD = D // H
        DL = 64
        LAMBDA_DECAY = 0.01
        b, s, d = x.shape
        q = x @ W_q
        k = x @ W_k
        v = x @ W_v
        latent_kv = (k + v) @ W_down_kv
        k_rec = (latent_kv @ W_up_k).reshape(b, s, H, HD).transpose(0, 2, 1, 3)
        v_rec = (latent_kv @ W_up_v).reshape(b, s, H, HD).transpose(0, 2, 1, 3)
        qh = q.reshape(b, s, H, HD).transpose(0, 2, 1, 3)
        scores = jnp.einsum('bhqd,bhkd->bhqk', qh, k_rec) / math.sqrt(d)
        t = jnp.arange(s, dtype=jnp.float32)
        decay = jnp.exp(-LAMBDA_DECAY * jnp.abs(t[:, None] - t[None, :]))
        scores = scores * decay[None, None, :, :]
        attn = jax.nn.softmax(scores, axis=-1)
        out = jnp.einsum('bhqk,bhkd->bhqd', attn, v_rec)
        out = out.transpose(0, 2, 1, 3).reshape(b, s, d)
        return out @ W_o

    def _L0_ffn_ref(hidden_states, gate_w, Wg, Wu, Wd, Sg, Su, Sd):
        import jax, jax.numpy as jnp
        import numpy as np
        E = 16
        F_C = 2.0
        D = 256
        I = 4 * D
        IS = 2 * D
        B, S = (4, 256)
        b, s, d = hidden_states.shape
        T = b * s
        C = int(T * F_C / E)
        flat_x = hidden_states.reshape(T, d)
        logits = flat_x @ gate_w.T
        scores = jax.nn.softmax(logits, axis=-1).T
        topk_weight, topk_idx = jax.lax.top_k(scores, C)
        xg = flat_x[topk_idx]
        g = jnp.einsum('ecd,eid->eci', xg, Wg)
        u = jnp.einsum('ecd,eid->eci', xg, Wu)
        h = jax.nn.gelu(g, approximate=False) * u
        eo = jnp.einsum('eci,edi->ecd', h, Wd)
        eo = eo * topk_weight[..., None]
        flat_out = jnp.zeros_like(flat_x).at[topk_idx.reshape(-1)].add(eo.reshape(-1, d))
        out = flat_out.reshape(b, s, d)
        sg = hidden_states @ Sg.T
        su = hidden_states @ Su.T
        shared = jax.nn.gelu(sg, approximate=False) * su @ Sd.T
        return out + shared
    h = _L0_tok_ref(x, L0_tok_conv_w, L0_tok_conv_b, L0_tok_ln_gamma, L0_tok_ln_beta)
    h = h + _L0_attn_ref(_layernorm(h, axis=-1), L0_attn_W_q, L0_attn_W_k, L0_attn_W_v, L0_attn_W_o, L0_attn_W_down_kv, L0_attn_W_up_k, L0_attn_W_up_v)
    h = h + _L0_ffn_ref(_layernorm(h, axis=-1), L0_ffn_gate_w, L0_ffn_Wg, L0_ffn_Wu, L0_ffn_Wd, L0_ffn_Sg, L0_ffn_Su, L0_ffn_Sd)
    return h

_drawn_inputs = setup_inputs


def setup_inputs(seed=0):
    import zlib

    import numpy as np

    out = dict(_drawn_inputs(seed))
    spreads = {'L0_tok_conv_b': (0.0, 0.1), 'L0_tok_ln_gamma': (1.0, 0.2), 'L0_tok_ln_beta': (0.0, 0.1)}
    factors = {'L0_ffn_gate_w': 8.0,
     'L0_ffn_Wg': 8.0,
     'L0_ffn_Wu': 8.0,
     'L0_ffn_Wd': 8.0,
     'L0_ffn_Sg': 8.0,
     'L0_ffn_Su': 8.0,
     'L0_ffn_Sd': 8.0}
    for name, (base, spread) in spreads.items():
        noise = np.random.default_rng([zlib.crc32(name.encode()), seed]).standard_normal(out[name].shape)
        drawn = base * np.exp(spread * noise) if base else spread * noise
        out[name] = jnp.asarray(drawn.astype(out[name].dtype))
    for name, factor in factors.items():
        out[name] = (out[name] * factor).astype(out[name].dtype)
    return out
```

```python
import numpy as np
import concourse.bass as bass
from concourse import mybir
from contextlib import ExitStack

F32, F16, I32 = mybir.dt.float32, mybir.dt.float16, mybir.dt.int32
ALU = mybir.AluOpType
ACT = mybir.ActivationFunctionType
AX = mybir.AxisListType

B, S, D = 32, 188, 256
HT = S // 2
TILES = 2 * B
T = B * S
NH, HD = 16, 16
E, CAP = 16, 2 * T // 16
FF, SF = 4 * D, 2 * D
DL = 64
ROW = D + E
WSCALE = 64.0
HSCALE = 4.0
EPS = 1e-5
CH = T // 8
NJ = CH // HT
SLOT_A, SLOT_B = 24, 32
SLOT_TILES = 6
GROUP = 4
CHUNK = 2 * S

C_ID, C_ONES, C_LOW, C_DECAY = 0, 128, 256, 384
C_MASK = C_DECAY + 2 * S
C_TOK = C_MASK + 8
C_BIT = C_TOK + 2 * 64
C_EPS = C_BIT + 32
C_IOTA = C_EPS + 1
C_ALL = C_IOTA + 32

W_CONV, W_Q, W_K, W_V, W_O = 0, 1024, 1536, 2048, 2560
W_GATE = 3072
W_SG = W_GATE + 2 * E
W_SU, W_SD = W_SG + 2 * SF, W_SG + 4 * SF
W_ALL = W_SD + 4 * D


class Chain:

    def __init__(self, eng, sem):
        self.eng, self.sem, self.base, self.n = eng, sem, 0, 0

    def link(self, ins):
        self.mark(ins)
        self.wait()

    def mark(self, ins):
        ins.then_inc(self.sem, 1)
        self.n += 1

    def wait(self):
        self.eng.wait_ge(self.sem, self.base + self.n)

    def enter(self, i, per):
        self.start, self.per, self.n = self.base + self.n, per, 0
        self.base = self.start + i * per

    def leave(self, trips):
        assert self.n == self.per, (self.n, self.per)
        self.base, self.n = self.start + trips * self.per, 0


def build(nc, x_t, conv_w, conv_b, gamma, beta, wq, wk_t, wv_t, wo, w_down, w_up_k, w_up_v, gate, s_g, s_u, s_d,
          e_g, e_u, e_d, const, out):
    xtab = nc.dram_tensor("token_table", (T, ROW), F32)
    sctab = nc.dram_tensor("score_table", (E, T), F32)
    ctx = ExitStack()
    with ctx:
        def sb(name, shape, dt=F32):
            return ctx.enter_context(nc.sbuf_tensor(name, shape, dt))

        def sem(name):
            return ctx.enter_context(nc.semaphore(name))

        bank = [ctx.enter_context(nc.psum_tensor(f"bank{i}", [128, 512], F32)) for i in range(8)]

        C = sb("constants", [128, C_ALL])
        ident = C[:, C_ID:C_ID + 128]
        H = sb("hidden", [128, TILES, D])
        MV = sb("mean_var", [128, TILES, 2])
        RSTD = sb("rstd", [128, TILES, 1])
        WH = sb("weights_hi", [128, W_ALL], F16)
        WL = sb("weights_lo", [128, W_ALL], F16)
        ARENA = sb("arena", [128, 28500])

        class Place:
            def __init__(self, at=0):
                self.at = at

            def __call__(self, cols, dt=F32):
                words = cols if dt in (F32, I32) else (cols + 1) // 2
                v = ARENA[:, self.at:self.at + words]
                self.at += words
                assert self.at <= 28500, self.at
                return v if dt == F32 else v.bitcast(dt)

        at0 = Place()
        WS = at0(W_ALL)
        WKT, WVT = at0(512), at0(512)
        WDN, WUK, WUV = at0(128), at0(256), at0(256)
        M1 = at0(256)
        BIAS, GAM, BET = at0(D), at0(D), at0(D)
        XS = [at0(4 * S) for _ in range(2)]
        XH = [at0(4 * S, F16) for _ in range(2)]
        XL = [at0(4 * S, F16) for _ in range(2)]
        STAT = [at0(6) for _ in range(2)]
        AGGR = [at0(2) for _ in range(4)]
        LN = [at0(D) for _ in range(4)]
        SD = at0(TILES)
        at2 = Place()
        XN = at2(2 * D)
        XTH, XTL, QH, QL = (at2(2 * S, F16) for _ in range(4))
        QMH = [at2(16 * S, F16) for _ in range(2)]
        QML = [at2(16 * S, F16) for _ in range(2)]
        KH = [at2(2 * S, F16) for _ in range(2)]
        KL = [at2(2 * S, F16) for _ in range(2)]
        V = [at2(2 * NH * (HD + 1)) for _ in range(2)]
        SC = [at2(2 * S) for _ in range(2)]
        P = [at2(2 * S) for _ in range(2)]
        PT = [at2(2 * S) for _ in range(2)]
        MAX, NEG = at2(2 * NH), at2(2 * NH)
        RS, ON = at2(2 * NH), at2(2 * D)
        OTH, OTL = at2(2 * S, F16), at2(2 * S, F16)
        AGGR2 = at2(4)
        STAT2 = [at2(6) for _ in range(2)]

        at3 = Place()
        XTOK = {"hi": at3(2 * T, F16), "lo": at3(2 * T, F16)}
        TOKH, TOKL = (v.rearrange("p (c n) -> p c n", c=2) for v in XTOK.values())
        at4 = Place(at3.at)
        ROWS = [at3(2 * GROUP * ROW) for _ in range(2)]
        LMAX, LSUM, LINV = at3(8), at3(8), at3(8)
        LEXP = at3(8 * E)
        SD2 = at3(TILES)
        SCT = [at3(2 * GROUP * HT) for _ in range(2)]
        SC8 = at4(CH)
        HIT = at4(CH)
        BITI, THR, CAND, GAIN, COUNT = at4(32, I32), at4(1, I32), at4(1, I32), at4(1, I32), at4(1)
        search_end = at4.at
        SGEL, SHF = [at4(CHUNK) for _ in range(2)], [at4(CHUNK) for _ in range(2)]
        SHH = [at4(4 * CHUNK, F16) for _ in range(2)]
        SHL = [at4(4 * CHUNK, F16) for _ in range(2)]
        SOUT = [at4(4 * D) for _ in range(2)]
        at5 = Place()
        QE = 4
        QC = QE * 64
        BO = [at5(SLOT_B * QC, F16) for _ in range(2)]
        assert at5.at <= at4.at
        at5 = Place(search_end)
        ONE, EQ, RANK = at5(CH), at5(CH), at5(CH)
        CGT, CEQ, NEED, LASTC, OFF = at5(1), at5(1), at5(1), at5(1), at5(1)
        SLF = at5(8 * 128)
        SLI, SAI = at5(8 * 128, I32), at5(8 * 128, I32)
        A16, B16, TH16, TL16 = (at5(8 * 128, F16) for _ in range(4))
        I32T, ILOW = at5(E * SLOT_A), at5(E * SLOT_A)
        HW = H[:, :, :].rearrange("p t n -> p (t n)")
        AO = [HW[:, i * 24 * QC:(i + 1) * 24 * QC].bitcast(F16) for i in range(2)]
        IDX = sb("slot_tokens", [128, E, SLOT_TILES], I32)
        WEH = [HW[:, i * 3072:(i + 1) * 3072].bitcast(F16) for i in range(2)]
        WEL = [HW[:, 6144 + i * 3072:6144 + (i + 1) * 3072].bitcast(F16) for i in range(2)]
        EO = [HW[:, 12288 + i * 1536:12288 + (i + 1) * 1536] for i in range(2)]
        at6 = Place()
        WST = at6(3 * 2048)
        XG = [at6(SLOT_TILES * ROW) for _ in range(2)]
        XGH, XGL = at6(2 * CAP, F16), at6(2 * CAP, F16)
        HEH, HEL = at6(8 * CAP, F16), at6(8 * CAP, F16)
        EGEL, EHF = [at6(CHUNK) for _ in range(2)], [at6(CHUNK) for _ in range(2)]
        IDXS = [at6(SLOT_TILES, I32) for _ in range(2)]
        WT = [at6(SLOT_TILES) for _ in range(2)]

        engines_met = sem("engines_met")
        block = ctx.enter_context(nc.Block())
        met = {}

        def meet(eng):
            eng.drain().then_inc(engines_met, 1)
            met[id(eng)] = met.get(id(eng), 0) + 5
            eng.wait_ge(engines_met, met[id(eng)])

        const_in, weights_in, fold_in = sem("const_in"), sem("weights_in"), sem("fold_in")
        summed, half_added = sem("kv_summed"), sem("half_added")
        m1_done, m1_copied, fold_done, fold_copied = sem("m1_done"), sem("m1_copied"), sem("fold_done"), sem("fold_copied")
        hi_done, lo_done = sem("w_hi_done"), sem("w_lo_done")
        x_in = [sem("x_in0"), sem("x_in1")]
        xh_ready, xl_ready = sem("xh_ready"), sem("xl_ready")
        conv_done, conv_free, dve1 = sem("conv_done"), sem("conv_free"), sem("dve1")
        sd_done, norm_done, gam_done, bet_done, stat_done = (
            sem("sd_done"), sem("norm_done"), sem("gamma_done"), sem("beta_done"), sem("stat_done"))
        dve_ln, sd2_done, rstd_done = sem("dve_ln"), sem("sd2_done"), sem("rstd_done")

        def split3(hi_a, lo_a, hi_b, lo_b):
            return ((hi_a, hi_b), (lo_a, hi_b), (hi_a, lo_b))

        scaled, exp_done, transposed, pv_done = sem("scaled+2"), sem("exp_done+2"), sem("transposed+2"), sem("pv_done+2")
        s_done = sem("scores_done")
        pt_ready = [sem("pt_even+1"), sem("pt_odd+1")]
        dve2 = sem("dve2")
        on_ready, ot_done, oth_ready, otl_ready, y_done, y_added = (
            sem(n) for n in ("on_ready", "ot_done", "oth_ready", "otl_ready", "y_done", "y_added"))
        xn_ready, xt_done, xth_ready, xtl_ready = (sem(n) for n in ("xn_ready", "xt_done", "xth_ready", "xtl_ready"))
        q_done, qh_ready, ql_ready, qm_ready = (sem(n) for n in ("q_done", "qh_ready", "ql_ready", "qm_ready"))
        k_done, kh_ready, kl_ready, v_done, v_ready = (
            sem(n) for n in ("k_done", "kh_ready", "kl_ready", "v_done", "v_ready"))
        ones_set = sem("v_ones_set")
        SBK, TBK, WBK, OBK = bank[0:2], bank[2:4], bank[4:6], bank[6:8]
        STEPS = NH + 3

        def batches(eng, body):
            body(0, 0, True, False)
            with eng.Fori(0, B // 2 - 1) as i:
                body(2 * i + 1, 1, False, False)
                body(2 * i + 2, 0, False, False)
            body(B - 1, 1, False, True)

        def hsplit(ap):
            return ap.rearrange("p (t n) -> p t n", t=2)

        row_ready, rt_done, rth_ready, rtl_ready = sem("row_ready"), sem("rt_done"), sem("rth_ready"), sem("rtl_ready+2")
        lg_done, lmax_done, lsub_done, lexp_done = sem("lg_done"), sem("lmax_done"), sem("lsub_done"), sem("lexp_done")
        lsum_done, score_ready, sct_done, sct_ready = sem("lsum_done"), sem("score_ready"), sem("sct_done"), sem("sct_ready")
        rstd2_in, rstd2_done = sem("sd_of_h1"), sem("rstd_of_h1")
        table_out = [sem("table_out0+32"), sem("table_out1+32")]
        sc8_in, gu_done, gel_ready, hf_ready, hh_ready, hl_ready = (
            sem(n) for n in ("sc8_in", "gu_done", "gel_ready", "hf_ready+2", "hh_ready", "hl_ready+2"))
        down_done, sh_added = sem("down_done"), sem("sh_added+2")
        sh_out = [sem("sh_out0+16"), sem("sh_out1+16")]
        search, count_ready, total_done = sem("search"), sem("count_ready"), sem("total_done")
        slots, gt_total, offs_done, slot_t_done, hot_ready, hot_used, hot_lo = (
            sem(n) for n in ("slots", "gt_total", "offs_done", "slot_t_done", "hot_ready", "hot_used", "hot_lo"))
        idx_done, idx_moved, ones_ready = sem("idx_done"), sem("idx_moved"), sem("ones_ready")
        w_in = [sem(f"w_in{i}") for i in range(3)]
        wh_ready = [sem(f"wh_ready{i}") for i in range(3)]
        wl_ready = [sem(f"wl_ready{i}") for i in range(3)]
        idx_ready, xg_in, xg_set = sem("idx_ready"), [sem("xg_in0"), sem("xg_in1")], sem("xg_set")
        xgt_done, xgh_ready, xgl_ready = sem("xgt_done"), sem("xgh_ready"), sem("xgl_ready+2")
        egu_done, egel_ready, ehf_ready, ehh_ready, ehl_ready = (
            sem(n) for n in ("egu_done", "egel_ready", "ehf_ready+2", "ehh_ready", "ehl_ready+2"))
        edown_done, eo_ready, scattered, wt_ready = sem("edown_done"), sem("eo_ready+2"), sem("scattered"), sem("wt_ready")
        ROWS3 = [v.rearrange("p (t n) -> p t n", n=ROW) for v in ROWS]
        GB = 8
        KS = T // CHUNK

        def pairs(eng, n, body):
            with eng.Fori(0, n // 2) as i:
                body(2 * i, 0)
                body(2 * i + 1, 1)

        def experts_loop(eng, body):
            body(0, 0, True, False)
            with eng.Fori(0, E // 2 - 1) as i:
                body(2 * i + 1, 1, False, False)
                body(2 * i + 2, 0, False, False)
            body(E - 1, 1, False, True)

        def slot_rows(m):
            return 128 if m < SLOT_TILES - 1 else CAP - 128 * (SLOT_TILES - 1)

        def token_columns(k):
            return bass.ts(k, CHUNK)

        passed = sem("waits_passed")

        def hold(eng):
            eng.sem_inc(passed, 1)

        @block.sync
        def _(sp):
            sp.dma_start(C[:, :], const).then_inc(const_in, 16)
            for dst, src in ((WKT, wk_t), (WVT, wv_t), (WDN, w_down)):
                sp.dma_start(dst.rearrange("p (c n) -> p c n", c=2), src.rearrange("(c p) n -> p c n", p=128)).then_inc(fold_in, 16)
            sp.dma_start(WUK[0:DL, :], w_up_k).then_inc(fold_in, 16)
            sp.dma_start(WUV[0:DL, :], w_up_v).then_inc(fold_in, 16)
            sp.dma_start(WS[:, W_CONV:W_Q].rearrange("p (c n) -> p c n", c=4), conv_w.rearrange("(c p) n -> p c n", p=128)).then_inc(weights_in, 16)
            for o, src in ((W_Q, wq), (W_O, wo)):
                sp.dma_start(WS[:, o:o + 512].rearrange("p (c n) -> p c n", c=2), src.rearrange("(c p) n -> p c n", p=128)).then_inc(weights_in, 16)
            sp.dma_start(WS[:, W_GATE:W_SG].rearrange("p (c n) -> p c n", c=2), gate.rearrange("(c p) n -> p c n", p=128)).then_inc(weights_in, 16)
            for o, src, c in ((W_SG, s_g, 2), (W_SU, s_u, 2), (W_SD, s_d, 4)):
                sp.dma_start(WS[:, o:o + 1024].rearrange("p (c n) -> p c n", c=c), src.rearrange("(c p) n -> p c n", p=128)).then_inc(weights_in, 16)
            for dst, src in ((BIAS, conv_b), (GAM, gamma), (BET, beta)):
                sp.dma_start(dst, src.rearrange("(a n) -> a n", a=1).broadcast_to((128, D))).then_inc(weights_in, 16)
            sp.dma_start(XS[0], x_t[0, :, :]).then_inc(x_in[0], 16)
            sp.dma_start(XS[1], x_t[1, :, :]).then_inc(x_in[1], 16)
            with sp.Fori(1, B // 2) as i:
                for par in range(2):
                    sp.wait_ge(xl_ready, 2 * i + par - 1)
                    sp.dma_start(XS[par], x_t[2 * i + par, :, :]).then_inc(x_in[par], 16)
            meet(sp)
            meet(sp)
            meet(sp)
            def group(g, par):
                sp.wait_ge(score_ready, g + 1)
                hold(sp)
                sp.dma_start(xtab[bass.ts(g, 2 * GROUP * HT), :].rearrange("(t p) n -> p t n", p=HT), ROWS3[par][0:HT, :, :]).then_inc(table_out[par], 16)
                sp.wait_ge(sct_ready, g + 1)
                hold(sp)
                sp.dma_start(sctab[:, bass.ts(g, 2 * GROUP * HT)], SCT[par][0:E, :]).then_inc(table_out[par], 16)
            pairs(sp, GB, group)
            for par in range(2):
                sp.wait_ge(table_out[par], 32 * (GB // 2 + 1))
            meet(sp)
            sp.dma_start(SC8, sctab[:, :].rearrange("e (c n) -> (e c) n", c=8)).then_inc(sc8_in, 16)

            def chunk(k, par):
                sp.wait_ge(sh_added, 2 * k + 4)
                hold(sp)
                sp.dma_start(out[bass.ts(k, CHUNK), :].rearrange("(t p) n -> p t n", p=HT),
                             SOUT[par][0:HT, :].rearrange("p (t n) -> p t n", t=4)).then_inc(sh_out[par], 16)
            pairs(sp, KS, chunk)
            for par in range(2):
                sp.wait_ge(sh_out[par], 16 * (KS // 2 + 1))
            meet(sp)
            meet(sp)

            def load(e, i):
                src = (e_g, e_u, e_d)[i]
                sp.dma_start(WST[:, i * 2048:(i + 1) * 2048], src[e, :, :]).then_inc(w_in[i], 16)

            for i in range(3):
                load(0, i)
            with sp.Fori(1, E) as e:
                for i in range(3):
                    sp.wait_ge(wl_ready[i], e)
                    hold(sp)
                    load(e, i)
            meet(sp)

        @block.gpsimd
        def _(pool):
            with pool.Fori(0, B // 2) as i:
                for par in range(2):
                    pool.wait_ge(xh_ready, 2 * i + par + 1)
                    nc.gpsimd.tensor_tensor(XL[par], XS[par], XH[par], ALU.subtract).then_inc(xl_ready, 1)
            meet(pool)
            with pool.Fori(0, TILES // 4) as i:
                t = 4 * i
                for j in range(4):
                    pool.wait_ge(gam_done, t + j + 1)
                    nc.gpsimd.tensor_tensor(H[0:HT, t + j, :], LN[j][0:HT, :], BET[0:HT, :], ALU.add).then_inc(bet_done, 1)
            meet(pool)
            for par in range(2):
                ones = V[par][0:HT, :].rearrange("p (k d) -> p k d", d=HD + 1)[:, :, HD:HD + 1]
                nc.gpsimd.memset(ones, 1.0).then_inc(ones_set, 1)
            mask = C[:, C_MASK:C_MASK + 8].unsqueeze(2).broadcast_to((128, 8, S))

            def mask_heads(b, par):
                for ready, src, dst in ((qh_ready, QH, QMH), (ql_ready, QL, QML)):
                    pool.wait_ge(ready, b + 1)
                    for g in range(2):
                        last = nc.gpsimd.tensor_tensor(
                            dst[par][:, g * 8 * S:(g + 1) * 8 * S].rearrange("p (h n) -> p h n", h=8),
                            src[:, g * S:(g + 1) * S].unsqueeze(1).broadcast_to((128, 8, S)), mask, ALU.mult)
                last.then_inc(qm_ready, 1)

            mask_heads(0, 0)

            def batch(b, par, first, last):
                if not last:
                    mask_heads(b + 1, 1 - par)
            batches(pool, batch)
            meet(pool)
            meet(pool)

            def low_hidden(dst, f, hi, ready_in, count, ready):
                pool.wait_ge(ready_in, count)
                nc.gpsimd.tensor_tensor(dst, f, hi, ALU.subtract).then_inc(ready, 1)

            def chunk(k, par):
                for m in range(4):
                    c = slice(m * CHUNK, (m + 1) * CHUNK)
                    low_hidden(SHL[par][:, c], SHF[m % 2], SHH[par][:, c], hh_ready, 4 * k + m + 1, hl_ready)
            pool.sem_inc(hl_ready, 2)
            pairs(pool, KS, chunk)
            meet(pool)
            nc.gpsimd.memset(ONE, 1.0).then_inc(ones_ready, 1)
            meet(pool)
            pool.sem_inc(ehl_ready, 2)
            for par in range(2):
                nc.gpsimd.memset(XG[par], 0.0).then_inc(xg_set, 1)
            pool.wait_ge(xg_set, 2)

            def gather(e, par):
                hold(pool)
                nc.gpsimd.tensor_copy(IDXS[par], IDX[:, e, :]).then_inc(idx_ready, 1)
                pool.wait_ge(idx_ready, e + 1)
                hold(pool)
                for m in range(SLOT_TILES):
                    n = slot_rows(m)
                    nc.gpsimd.indirect_dma_start(
                        XG[par][0:n, m * ROW:(m + 1) * ROW], None, xtab[:, :],
                        bass.IndirectOffsetOnAxis(ap=IDXS[par][0:n, m:m + 1], axis=0)).then_inc(xg_in[par], 16)

            def scatter(e, par):
                for m in range(SLOT_TILES):
                    n = slot_rows(m)
                    pool.wait_ge(eo_ready, 6 * e + m + 3)
                    hold(pool)
                    nc.gpsimd.indirect_dma_start(
                        out[:, :], bass.IndirectOffsetOnAxis(ap=IDXS[par][0:n, m:m + 1], axis=0),
                        EO[par][0:n, m * D:(m + 1) * D], None, compute_op=ALU.add).then_inc(scattered, 16)

            def expert(e, par, first, last):
                for n in range(2):
                    for m in range(8):
                        s = 8 * n + m
                        if s == 2 and not first:
                            scatter(e - 1, 1 - par)
                        if s == 3 and not last:
                            if not first:
                                pool.wait_ge(scattered, 96 * e)
                            gather(e + 1, 1 - par)
                        c = slice(m * CAP + n * CHUNK, m * CAP + (n + 1) * CHUNK)
                        low_hidden(HEL[:, c], EHF[s % 2], HEH[:, c], ehh_ready, 16 * e + s + 1, ehl_ready)

            gather(0, 0)
            experts_loop(pool, expert)
            pool.wait_ge(scattered, 96 * (E - 1))
            scatter(E - 1, 1)
            pool.wait_ge(scattered, 96 * E)
            meet(pool)

        @block.scalar
        def _(act):
            def copy(dst, src, scale=1.0):
                return nc.scalar.activation(dst, src, ACT.Copy, scale=scale)

            act.sem_inc(exp_done, 2)
            act.sem_inc(pt_ready[0], 1)
            act.wait_ge(m1_done, 1)
            copy(M1[0:DL, :], bank[0][0:DL, 0:256]).then_inc(m1_copied, 1)
            for i in range(2):
                act.wait_ge(fold_done, i + 1)
                copy(WS[:, W_K + 512 * i:W_K + 512 * (i + 1)], bank[2 + i][:, :]).then_inc(fold_copied, 1)
            act.wait_ge(weights_in, 16 * 10)
            act.wait_ge(half_added, 4)
            act.wait_ge(fold_copied, 2)
            copy(WH[:, :], WS, WSCALE).then_inc(hi_done, 1)
            with act.Fori(0, B // 2) as i:
                for par in range(2):
                    act.wait_ge(x_in[par], 16 * i + 16)
                    act.wait_ge(conv_done, 4 * i + 2 * par + 2)
                    copy(XH[par], XS[par]).then_inc(xh_ready, 1)
            meet(act)
            nc.scalar.activation(SD[0:HT, :], MV[0:HT, :, 1], ACT.Sqrt, bias=C[0:HT, C_EPS:C_EPS + 1]).then_inc(sd_done, 1)
            act.wait_ge(stat_done, 3 * TILES)
            nc.scalar.activation(SD[0:HT, :], MV[0:HT, :, 1], ACT.Sqrt, bias=C[0:HT, C_EPS:C_EPS + 1]).then_inc(sd2_done, 1)
            meet(act)

            def project_halves(b, par, stage):
                if stage == "x":
                    act.wait_ge(xt_done, b + 1)
                    copy(XTH, WBK[0][:, 0:2 * S]).then_inc(xth_ready, 1)
                elif stage == "q":
                    act.wait_ge(q_done, b + 1)
                    if not isinstance(b, int) or b > 0:
                        act.wait_ge(qm_ready, b)
                    copy(QH, WBK[1][:, 0:2 * S]).then_inc(qh_ready, 1)
                elif stage == "k":
                    act.wait_ge(k_done, b + 1)
                    copy(KH[par], WBK[0][:, 0:2 * S]).then_inc(kh_ready, 1)
                else:
                    act.wait_ge(v_done, b + 1)
                    act.wait_ge(ones_set, 2)
                    for kt in range(2):
                        src = WBK[1][0:HT, kt * D:(kt + 1) * D].rearrange("p (h d) -> p h d", d=HD)
                        dst = hsplit(V[par][0:HT, :])[:, kt, :].rearrange("p (h d) -> p h d", d=HD + 1)[:, :, 0:HD]
                        last = copy(dst, src, 1.0 / WSCALE)
                    last.then_inc(v_ready, 1)

            def out_half(b):
                act.wait_ge(ot_done, b + 1)
                copy(OTH, WBK[0][:, 0:2 * S]).then_inc(oth_ready, 1)

            def batch(b, par, first, last):
                n = b * NH
                for s in range(STEPS):
                    if s < NH:
                        act.wait_ge(scaled, n + s + 3)
                        act.wait_ge(transposed, n + s + 1)
                        for qt in range(2):
                            ins = nc.scalar.activation(P[s % 2][0:HT, qt * S:(qt + 1) * S], SC[s % 2][0:HT, qt * S:(qt + 1) * S],
                                                       ACT.Exp, bias=NEG[0:HT, qt * NH + s:qt * NH + s + 1])
                        ins.then_inc(exp_done, 1)
                    if s == 2 and not first:
                        out_half(b - 1)
                    if not last:
                        for at, stage in ((6, "x"), (8, "q"), (10, "k"), (12, "v")):
                            if s == at:
                                project_halves(b + 1, 1 - par, stage)
                    h = s - 2
                    if 0 <= h < NH and h % 2 == 0:
                        act.wait_ge(transposed, n + h + 3)
                        act.wait_ge(pv_done, n + h + 1)
                        copy(PT[0][0:HT, :], TBK[0][0:HT, 0:2 * S]).then_inc(pt_ready[0], 1)

            for stage in "xqkv":
                project_halves(0, 0, stage)
            batches(act, batch)
            out_half(B - 1)
            meet(act)

            nc.scalar.activation(SD2[0:HT, :], MV[0:HT, :, 1], ACT.Sqrt, bias=C[0:HT, C_EPS:C_EPS + 1]).then_inc(rstd2_in, 1)

            def group(g, par):
                for j in range(GROUP):
                    act.wait_ge(rt_done, GROUP * g + j + 1)
                    hold(act)
                    copy(TOKH[:, :, bass.ts(GROUP * g + j, S)], WBK[j % 2][:, 0:2 * S].rearrange("p (c n) -> p c n", c=2)).then_inc(rth_ready, 1)
                act.wait_ge(lsub_done, g + 1)
                nc.scalar.activation(LEXP[0:HT, :], LEXP[0:HT, :], ACT.Exp, scale=1.0 / WSCALE).then_inc(lexp_done, 1)
                act.wait_ge(sct_done, g + 1)
                act.wait_ge(table_out[par], 16 * g + 32 - 16 * par)
                for i in range(2):
                    last = copy(SCT[par][0:E, i * 376:(i + 1) * 376], bank[6 + i][0:E, 0:376])
                last.then_inc(sct_ready, 1)
            pairs(act, GB, group)
            meet(act)

            def chunk(k, par):
                for m in range(5):
                    if m < 4:
                        act.wait_ge(gu_done, 4 * k + m + 1)
                        act.wait_ge(hf_ready, 4 * k + m + 1)
                        nc.scalar.activation(SGEL[m % 2], bank[2 * (m % 2)][:, 0:CHUNK], ACT.Gelu, scale=1.0 / WSCALE).then_inc(gel_ready, 1)
                    if m > 0:
                        act.wait_ge(hf_ready, 4 * k + m + 2)
                        copy(SHH[par][:, (m - 1) * CHUNK:m * CHUNK], SHF[(m - 1) % 2]).then_inc(hh_ready, 1)
            pairs(act, KS, chunk)
            meet(act)
            meet(act)

            def high_weights(e, i, par):
                act.wait_ge(w_in[i], 16 * e + 16)
                c = slice(i * 2048, (i + 1) * 2048)
                copy(WEH[par][:, c], WST[:, c], WSCALE).then_inc(wh_ready[i], 1)

            def high_tokens(e):
                for i in range(4):
                    act.wait_ge(xgt_done, 4 * e + i + 1)
                    c, t0, n = i % 2, 512 * (i // 2), (512, CAP - 512)[i // 2]
                    copy(XGH[:, c * CAP + t0:c * CAP + t0 + n], bank[6 + c][:, 0:n]).then_inc(xgh_ready, 1)

            def expert(e, par, first, last):
                for s in range(17):
                    if s < 16:
                        act.wait_ge(egu_done, 16 * e + s + 1)
                        act.wait_ge(ehf_ready, 16 * e + s + 1)
                        nc.scalar.activation(EGEL[s % 2], bank[2 * (s % 2)][:, 0:CHUNK], ACT.Gelu, scale=1.0 / WSCALE).then_inc(egel_ready, 1)
                    if s > 0:
                        n, m = (s - 1) // 8, (s - 1) % 8
                        act.wait_ge(ehf_ready, 16 * e + s + 2)
                        copy(HEH[:, m * CAP + n * CHUNK:m * CAP + (n + 1) * CHUNK], EHF[(s - 1) % 2]).then_inc(ehh_ready, 1)
                    if s in (3, 7, 11) and not last:
                        high_weights(e + 1, (s - 3) // 4, 1 - par)
                if not last:
                    high_tokens(e + 1)

            for i in range(3):
                high_weights(0, i, 0)
            high_tokens(0)
            experts_loop(act, expert)
            meet(act)

        @block.vector
        def _(dve):
            for s_, v_ in ((conv_free, 2), (scaled, 2), (pt_ready[1], 1)):
                dve.sem_inc(s_, v_)
            dve.wait_ge(fold_in, 16 * 5)
            nc.vector.tensor_tensor(WKT, WKT, WVT, ALU.add).then_inc(summed, 1)
            dve.wait_ge(weights_in, 16 * 10)
            dve.wait_ge(const_in, 16)
            for c in range(4):
                half = WS[:, W_CONV + 256 * c + 128 * (c % 2):W_CONV + 256 * c + 128 * (c % 2) + 128]
                nc.vector.scalar_tensor_tensor(half, ident, 0.5, half, ALU.mult, ALU.add).then_inc(half_added, 1)
            dve.wait_ge(hi_done, 1)
            nc.vector.scalar_tensor_tensor(WL[:, :], WS, WSCALE, WH[:, :], ALU.mult, ALU.subtract).then_inc(lo_done, 1)

            chain = Chain(dve, dve1)
            with dve.Fori(0, B // 2) as i:
                chain.enter(i, 16)
                for par in range(2):
                    for qt in range(2):
                        t = 4 * i + 2 * par + qt
                        dve.wait_ge(conv_done, t + 5)
                        chain.link(nc.vector.scalar_tensor_tensor(
                            H[0:HT, t, :], bank[2 * par + qt][0:HT, 0:D], 1.0 / WSCALE, BIAS[0:HT, :], ALU.mult, ALU.add))
                        hold(dve)
                        chain.link(nc.vector.bn_stats(STAT[qt][0:HT, :], H[0:HT, t, :]))
                        hold(dve)
                        chain.link(nc.vector.bn_aggr(AGGR[qt][0:HT, :], STAT[qt][0:HT, :]))
                        chain.mark(nc.vector.tensor_copy(MV[0:HT, t, :], AGGR[qt][0:HT, :]))
                    dve.sem_inc(conv_free, 1)
            chain.leave(B // 2)
            meet(dve)
            chain = Chain(dve, dve_ln)
            dve.wait_ge(sd_done, 1)
            chain.link(nc.vector.reciprocal(RSTD[0:HT, :, 0], SD[0:HT, :]))

            def stats(t, j, sems, count):
                hold(dve)
                nc.vector.bn_stats(STAT[j % 2][0:HT, :], H[0:HT, t, :]).then_inc(sems, 1)
                dve.wait_ge(sems, count)
                hold(dve)
                nc.vector.bn_aggr(AGGR[j][0:HT, :], STAT[j % 2][0:HT, :]).then_inc(sems, 1)
                dve.wait_ge(sems, count + 1)
                nc.vector.tensor_copy(MV[0:HT, t, :], AGGR[j][0:HT, :]).then_inc(sems, 1)

            def normed(t, j):
                nc.vector.tensor_scalar(LN[j][0:HT, :], H[0:HT, t, :], MV[0:HT, t, 0:1], RSTD[0:HT, t, :],
                                        ALU.subtract, ALU.mult).then_inc(norm_done, 1)
                dve.wait_ge(norm_done, t + 1)
                nc.vector.tensor_tensor(LN[j][0:HT, :], LN[j][0:HT, :], GAM[0:HT, :], ALU.mult).then_inc(gam_done, 1)

            def stats_of(t, j):
                dve.wait_ge(bet_done, t + 1)
                stats(t, j, stat_done, 3 * t + 1)

            for j in range(4):
                normed(j, j)
            with dve.Fori(0, TILES // 4 - 1) as i:
                t = 4 * i
                for j in range(4):
                    stats_of(t + j, j)
                    normed(t + 4 + j, j)
            for j in range(4):
                stats_of(TILES - 4 + j, j)
            dve.wait_ge(sd2_done, 1)
            nc.vector.reciprocal(RSTD[0:HT, :, 0], SD[0:HT, :]).then_inc(rstd_done, 1)
            meet(dve)
            def x_norm(b):
                for qt in range(2):
                    t = 2 * b + qt
                    last = nc.vector.tensor_scalar(XN[0:HT, qt * D:(qt + 1) * D], H[0:HT, t, :], MV[0:HT, t, 0:1],
                                                   RSTD[0:HT, t, :], ALU.subtract, ALU.mult)
                last.then_inc(xn_ready, 1)

            def low(dst, src, hi, hi_ready, count, ready):
                dve.wait_ge(hi_ready, count)
                nc.vector.tensor_tensor(dst, src, hi, ALU.subtract).then_inc(ready, 1)

            def project_halves(b, par, stage):
                if stage == "n":
                    x_norm(b)
                elif stage == "x":
                    low(XTL, WBK[0][:, 0:2 * S], XTH, xth_ready, b + 1, xtl_ready)
                elif stage == "q":
                    low(QL, WBK[1][:, 0:2 * S], QH, qh_ready, b + 1, ql_ready)
                else:
                    low(KL[par], WBK[0][:, 0:2 * S], KH[par], kh_ready, b + 1, kl_ready)

            def add_out(b):
                dve.wait_ge(y_done, b + 1)
                both = H[0:HT, bass.ts(b, 2), :].rearrange("p t n -> p (t n)")
                nc.vector.scalar_tensor_tensor(both, WBK[1][0:HT, 0:2 * D], 1.0 / WSCALE, both, ALU.mult, ALU.add).then_inc(y_added, 1)
                dve.wait_ge(y_added, b + 1)
                hold(dve)
                for qt in range(2):
                    nc.vector.bn_stats(STAT2[qt][0:HT, :], H[0:HT, 2 * b + qt, :]).then_inc(dve2, 1)
                dve.wait_ge(dve2, 5 * b + 2)
                hold(dve)
                for qt in range(2):
                    nc.vector.bn_aggr(AGGR2[0:HT, 2 * qt:2 * qt + 2], STAT2[qt][0:HT, :]).then_inc(dve2, 1)
                dve.wait_ge(dve2, 5 * b + 4)
                nc.vector.tensor_copy(MV[0:HT, bass.ts(b, 2), :], hsplit(AGGR2[0:HT, :])).then_inc(dve2, 1)

            head_max = sem("head_max")
            inv_done = sem("inv_done")

            def batch(b, par, first, last):
                n = b * NH
                for s in range(STEPS):
                    if s < NH:
                        dve.wait_ge(s_done, n + s + 1)
                        dve.wait_ge(exp_done, n + s + 1)
                        hold(dve)
                        for qt in range(2):
                            nc.vector.tensor_tensor_reduce(
                                out=SC[s % 2][0:HT, qt * S:(qt + 1) * S], in0=SBK[s % 2][0:HT, qt * S:(qt + 1) * S],
                                in1=C[0:HT, C_DECAY + qt * S:C_DECAY + (qt + 1) * S], scale=1.0, scalar=-3e38,
                                op0=ALU.mult, op1=ALU.max, accum_out=MAX[0:HT, qt * NH + s:qt * NH + s + 1]).then_inc(head_max, 1)
                        dve.wait_ge(head_max, 2 * (n + s + 1))
                        nc.vector.tensor_scalar(NEG[0:HT, s::NH], MAX[0:HT, s::NH], -1.0, None, ALU.mult).then_inc(scaled, 1)
                    if not first:
                        if s == 2:
                            low(OTL, WBK[0][:, 0:2 * S], OTH, oth_ready, b, otl_ready)
                        if s == 4:
                            add_out(b - 1)
                    if not last:
                        for at, stage in ((4, "n"), (6, "x"), (8, "q"), (10, "k")):
                            if s == at:
                                project_halves(b + 1, 1 - par, stage)
                    h = s - 2
                    if 0 <= h < NH and h % 2 == 1:
                        dve.wait_ge(transposed, n + h + 3)
                        dve.wait_ge(pv_done, n + h + 1)
                        nc.vector.tensor_copy(PT[1][0:HT, :], TBK[1][0:HT, 0:2 * S]).then_inc(pt_ready[1], 1)
                dve.wait_ge(pv_done, n + NH + 2)
                for qt in range(2):
                    o = OBK[qt][0:HT, 0:NH * (HD + 1)].rearrange("p (h d) -> p h d", d=HD + 1)
                    nc.vector.reciprocal(RS[0:HT, qt * NH:(qt + 1) * NH], o[:, :, HD]).then_inc(inv_done, 1)
                dve.wait_ge(inv_done, 2 * (b + 1))
                for qt in range(2):
                    o = OBK[qt][0:HT, 0:NH * (HD + 1)].rearrange("p (h d) -> p h d", d=HD + 1)
                    last_ = nc.vector.tensor_tensor(
                        ON[0:HT, qt * D:(qt + 1) * D].rearrange("p (h d) -> p h d", d=HD), o[:, :, 0:HD],
                        RS[0:HT, qt * NH:(qt + 1) * NH].unsqueeze(2).broadcast_to((HT, NH, HD)), ALU.mult)
                last_.then_inc(on_ready, 1)

            for stage in "nxqk":
                project_halves(0, 0, stage)
            batches(dve, batch)
            low(OTL, WBK[0][:, 0:2 * S], OTH, oth_ready, B, otl_ready)
            add_out(B - 1)
            meet(dve)
            dve.sem_inc(rtl_ready, 2)
            for par in range(2):
                dve.sem_inc(table_out[par], 32)
            dve.wait_ge(rstd2_in, 1)
            nc.vector.reciprocal(RSTD[0:HT, :, 0], SD2[0:HT, :]).then_inc(rstd2_done, 1)
            dve.wait_ge(rstd2_done, 1)

            def group(g, par):
                dve.wait_ge(table_out[par], 16 * g + 32 - 16 * par)
                hold(dve)
                for j in range(GROUP):
                    for qt in range(2):
                        t = 2 * GROUP * g + 2 * j + qt
                        last = nc.vector.tensor_scalar(ROWS3[par][0:HT, 2 * j + qt, 0:D], H[0:HT, t, :], MV[0:HT, t, 0:1],
                                                       RSTD[0:HT, t, :], ALU.subtract, ALU.mult)
                    last.then_inc(row_ready, 1)
                for j in range(GROUP):
                    dve.wait_ge(rth_ready, GROUP * g + j + 1)
                    at = bass.ts(GROUP * g + j, S)
                    nc.vector.tensor_tensor(TOKL[:, :, at], WBK[j % 2][:, 0:2 * S].rearrange("p (c n) -> p c n", c=2),
                                            TOKH[:, :, at], ALU.subtract).then_inc(rtl_ready, 1)
                dve.wait_ge(lg_done, g + 1)
                logits = bank[2 + par][0:HT, 0:8 * E].rearrange("p (t n) -> p t n", n=E)
                exps = LEXP[0:HT, :].rearrange("p (t n) -> p t n", n=E)

                def spread(v):
                    return v[0:HT, :].unsqueeze(2).broadcast_to((HT, 8, E))
                nc.vector.tensor_reduce(LMAX[0:HT, :], logits, AX.X, ALU.max).then_inc(lmax_done, 1)
                dve.wait_ge(lmax_done, g + 1)
                nc.vector.tensor_tensor(exps, logits, spread(LMAX), ALU.subtract).then_inc(lsub_done, 1)
                dve.wait_ge(lexp_done, g + 1)
                nc.vector.tensor_reduce(LSUM[0:HT, :], exps, AX.X, ALU.add).then_inc(lsum_done, 1)
                dve.wait_ge(lsum_done, 2 * g + 1)
                nc.vector.reciprocal(LINV[0:HT, :], LSUM[0:HT, :]).then_inc(lsum_done, 1)
                dve.wait_ge(lsum_done, 2 * g + 2)
                nc.vector.tensor_tensor(ROWS3[par][0:HT, :, D:ROW], exps, spread(LINV), ALU.mult).then_inc(score_ready, 1)
            pairs(dve, GB, group)
            meet(dve)
            dve.sem_inc(hf_ready, 2)
            dve.sem_inc(sh_added, 2)
            for par in range(2):
                dve.sem_inc(sh_out[par], 16)
            find = Chain(dve, search)
            find.mark(nc.vector.tensor_copy(BITI, C[:, C_BIT:C_BIT + 32]))
            find.link(nc.vector.memset(THR, 0))
            dve.wait_ge(sc8_in, 16)

            def count(it):
                find.link(nc.vector.tensor_tensor(CAND, THR, BITI[:, bass.ds(it, 1)], ALU.bitwise_or))
                nc.vector.tensor_scalar(HIT, SC8, CAND.bitcast(F32), None, ALU.is_ge, ALU.add, accum_out=COUNT).then_inc(count_ready, 1)

            def decide(it):
                dve.wait_ge(total_done, it + 1)
                find.link(nc.vector.tensor_scalar(GAIN, bank[7][:, 0:1], float(CAP), C[:, bass.ds(C_BIT + it, 1)], ALU.is_ge, ALU.mult))
                find.link(nc.vector.tensor_tensor(THR, THR, GAIN, ALU.bitwise_or))

            def down_out(k, par, i):
                dve.wait_ge(down_done, 2 * k + i + 1)
                if i == 0:
                    dve.wait_ge(sh_out[par], 8 * k + 16 - 8 * par)
                nc.vector.scalar_tensor_tensor(
                    SOUT[par][0:HT, i * 2 * D:(i + 1) * 2 * D], bank[4 + i][0:HT, :], 1.0 / (WSCALE * HSCALE),
                    H[0:HT, bass.ts(2 * k + i, 2), :].rearrange("p t n -> p (t n)"), ALU.mult, ALU.add).then_inc(sh_added, 1)

            with dve.Fori(0, KS // 2) as i2:
                find.enter(i2, 12)
                for par in range(2):
                    k = 2 * i2 + par
                    for m in range(4):
                        if m % 2 == 0:
                            count(2 * k + m // 2)
                        dve.wait_ge(gel_ready, 4 * k + m + 1)
                        dve.wait_ge(hl_ready, 4 * k + m + 1)
                        nc.vector.scalar_tensor_tensor(SHF[m % 2], bank[2 * (m % 2) + 1][:, 0:CHUNK], HSCALE / WSCALE, SGEL[m % 2],
                                                       ALU.mult, ALU.mult).then_inc(hf_ready, 1)
                        if m % 2 == 1:
                            decide(2 * k + m // 2)
                    for i in range(2):
                        down_out(k, par, i)
            find.leave(KS // 2)
            meet(dve)
            step = Chain(dve, slots)
            thr = THR.bitcast(F32)
            nc.vector.tensor_scalar(HIT, SC8, thr, None, ALU.is_gt, ALU.add, accum_out=CGT).then_inc(slots, 1)
            step.n += 1
            step.link(nc.vector.tensor_scalar(EQ, SC8, thr, None, ALU.is_equal, ALU.add, accum_out=CEQ))
            dve.wait_ge(ones_ready, 1)
            step.mark(nc.vector.tensor_tensor_scan(RANK, ONE, EQ, 0.0, ALU.mult, ALU.add))
            dve.wait_ge(gt_total, 1)
            step.link(nc.vector.tensor_scalar(NEED, bank[0][:, 0:1], -1.0, float(CAP), ALU.mult, ALU.add))
            step.link(nc.vector.tensor_tensor(NEED, NEED, bank[1][:, 0:1], ALU.subtract))
            step.link(nc.vector.scalar_tensor_tensor(EQ, RANK, NEED, EQ, ALU.is_le, ALU.mult))
            step.link(nc.vector.tensor_tensor(HIT, HIT, EQ, ALU.add))
            step.link(nc.vector.tensor_tensor_scan(RANK, ONE, HIT, 0.0, ALU.mult, ALU.add))
            step.link(nc.vector.tensor_copy(LASTC, RANK[:, CH - 1:CH]))
            dve.wait_ge(offs_done, 1)
            step.link(nc.vector.tensor_copy(OFF, bank[2][:, 0:1]))
            step.link(nc.vector.scalar_tensor_tensor(RANK, RANK, OFF, HIT, ALU.add, ALU.mult))
            step.link(nc.vector.tensor_scalar(RANK, RANK, -1.0, None, ALU.add))
            dve.wait_ge(slot_t_done, 1)
            for i in range(2):
                step.mark(nc.vector.tensor_copy(SLI[0:HT, i * 512:(i + 1) * 512], bank[4 + i][0:HT, :]))
            step.wait()
            step.mark(nc.vector.tensor_scalar(SAI[0:HT, :], SLI[0:HT, :], 5, None, ALU.arith_shift_right))
            step.link(nc.vector.tensor_scalar(SLI[0:HT, :], SLI[0:HT, :], 31, None, ALU.bitwise_and))
            step.mark(nc.vector.tensor_copy(A16[0:HT, :], SAI[0:HT, :]))
            step.mark(nc.vector.tensor_copy(B16[0:HT, :], SLI[0:HT, :]))
            for i, dst in enumerate((TH16, TL16)):
                tok = C[0:HT, C_TOK + 64 * i:C_TOK + 64 * (i + 1)].rearrange("p (j c) -> p j c", c=8)
                step.mark(nc.vector.tensor_copy(dst[0:HT, :].rearrange("p (j e c) -> p j e c", e=E, c=8),
                                                tok.unsqueeze(2).broadcast_to((HT, NJ, E, 8))))
            step.wait()

            def quarter(v, q):
                return v[0:HT, :].rearrange("p (j w) -> p j w", j=NJ)[:, :, q * 8 * QE:(q + 1) * 8 * QE]

            for q in range(E // QE):
                par = q % 2
                if q >= 2:
                    dve.wait_ge(hot_used, q - 1)
                bo = BO[par][0:HT, :].rearrange("p (b j w) -> p b j w", b=SLOT_B, j=NJ)
                ao = AO[par][0:HT, :].rearrange("p (h a j w) -> p h a j w", h=2, a=SLOT_A, j=NJ)
                for b_ in range(SLOT_B):
                    last = nc.vector.tensor_scalar(bo[:, b_], quarter(B16, q), float(b_), None, ALU.is_equal)
                for a_ in range(SLOT_A):
                    for h_, tok in enumerate((TH16, TL16)):
                        last = nc.vector.scalar_tensor_tensor(ao[:, h_, a_], quarter(A16, q), float(a_), quarter(tok, q), ALU.is_equal, ALU.mult)
                last.then_inc(hot_ready, 1)
            dve.wait_ge(idx_done, 2)
            for i in range(2):
                src = bank[i][0:SLOT_B, 0:8 * 2 * SLOT_A].rearrange("p (e h a) -> p e h a", e=8, h=2)
                low_ = ILOW[0:SLOT_B, i * 192:(i + 1) * 192].rearrange("p (e a) -> p e a", e=8)
                step.link(nc.vector.tensor_copy(low_, src[:, :, 1]))
                step.link(nc.vector.tensor_tensor(I32T[0:SLOT_B, i * 192:(i + 1) * 192].rearrange("p (e a) -> p e a", e=8), src[:, :, 0], low_, ALU.add))
            for i in range(4):
                src = I32T[0:SLOT_B, :].rearrange("p (e m i) -> p e m i", e=E, i=4)
                step.mark(nc.vector.tensor_copy(IDX[32 * i:32 * i + 32, :, :], src[:, :, :, i]))
            meet(dve)
            dve.sem_inc(xgl_ready, 2)
            dve.sem_inc(ehf_ready, 2)
            dve.sem_inc(eo_ready, 2)

            def low_weights(e, i, par):
                dve.wait_ge(wh_ready[i], e + 1)
                c = slice(i * 2048, (i + 1) * 2048)
                nc.vector.scalar_tensor_tensor(WEL[par][:, c], WST[:, c], WSCALE, WEH[par][:, c],
                                               ALU.mult, ALU.subtract).then_inc(wl_ready[i], 1)

            def low_tokens(e, par):
                for i in range(4):
                    dve.wait_ge(xgh_ready, 4 * e + i + 1)
                    c, t0, n = i % 2, 512 * (i // 2), (512, CAP - 512)[i // 2]
                    w = slice(c * CAP + t0, c * CAP + t0 + n)
                    nc.vector.tensor_tensor(XGL[:, w], bank[6 + c][:, 0:n], XGH[:, w], ALU.subtract).then_inc(xgl_ready, 1)
                rows = XG[par].rearrange("p (m n) -> p m n", n=ROW)[:, :, bass.ds(D + e, 1)]
                nc.vector.tensor_scalar(WT[par].unsqueeze(2), rows, 1.0 / (WSCALE * HSCALE), None, ALU.mult).then_inc(wt_ready, 1)

            def expert(e, par, first, last):
                for s in range(16):
                    dve.wait_ge(egel_ready, 16 * e + s + 1)
                    dve.wait_ge(ehl_ready, 16 * e + s + 1)
                    nc.vector.scalar_tensor_tensor(EHF[s % 2], bank[2 * (s % 2) + 1][:, 0:CHUNK], HSCALE / WSCALE, EGEL[s % 2],
                                                   ALU.mult, ALU.mult).then_inc(ehf_ready, 1)
                    if s in (5, 9, 13) and not last:
                        low_weights(e + 1, (s - 5) // 4, 1 - par)
                if not last:
                    low_tokens(e + 1, 1 - par)
                dve.wait_ge(wt_ready, e + 1)
                for m in range(SLOT_TILES):
                    n = slot_rows(m)
                    dve.wait_ge(edown_done, 6 * e + m + 1)
                    nc.vector.tensor_scalar(EO[par][0:n, m * D:(m + 1) * D], bank[4 + m % 2][0:n, 0:D], WT[par][0:n, m:m + 1],
                                            None, ALU.mult).then_inc(eo_ready, 1)

            for i in range(3):
                low_weights(0, i, 0)
            low_tokens(0, 0)
            experts_loop(dve, expert)
            meet(dve)

        @block.tensor
        def _(pe):
            mm = nc.tensor.matmul
            for s_, v_ in ((conv_done, 4), (transposed, 2), (pv_done, 2)):
                pe.sem_inc(s_, v_)
            pe.wait_ge(summed, 1)
            for c in range(2):
                last = mm(bank[0][0:DL, 0:256], WDN[:, c * DL:(c + 1) * DL], WKT[:, c * 256:(c + 1) * 256], start=c == 0, stop=c == 1)
            last.then_inc(m1_done, 1)
            pe.wait_ge(m1_copied, 1)
            for i, up in enumerate((WUK, WUV)):
                for c in range(2):
                    last = mm(bank[2 + i][:, c * 256:(c + 1) * 256], M1[0:DL, c * 128:(c + 1) * 128], up[0:DL, :], start=True, stop=True)
                last.then_inc(fold_done, 1)
            pe.wait_ge(lo_done, 1)
            with pe.Fori(0, B // 2) as i:
                for par in range(2):
                    pe.wait_ge(xl_ready, 2 * i + par + 1)
                    pe.wait_ge(conv_free, 2 * i + par + 1)
                    for qt in range(2):
                        n = 0
                        for c in range(4):
                            w = slice(W_CONV + c * D, W_CONV + (c + 1) * D)
                            x = slice(c * S + qt * HT, c * S + (qt + 1) * HT)
                            for a, w_ in split3(XH[par][:, x], XL[par][:, x], WH[:, w], WL[:, w]):
                                last = mm(bank[2 * par + qt][0:HT, 0:D], a, w_, start=n == 0, stop=n == 11)
                                n += 1
                        last.then_inc(conv_done, 1)
            meet(pe)
            meet(pe)
            def project(b, par, stage, first):
                if stage == "x":
                    pe.wait_ge(xn_ready, b + 1)
                    for c in range(2):
                        for qt in range(2):
                            last = nc.tensor.transpose(WBK[0][:, c * S + qt * HT:c * S + (qt + 1) * HT],
                                                       XN[0:HT, qt * D + c * 128:qt * D + (c + 1) * 128], ident[0:HT, 0:HT])
                    last.then_inc(xt_done, 1)
                elif stage in "qk":
                    if stage == "q":
                        pe.wait_ge(xtl_ready, b + 1)
                        if not first:
                            pe.wait_ge(y_added, b - 1)
                    w0, dst, done = (W_Q, WBK[1], q_done) if stage == "q" else (W_K, WBK[0], k_done)
                    for g in range(2):
                        n = 0
                        for c in range(2):
                            w = slice(w0 + c * D + g * 128, w0 + c * D + (g + 1) * 128)
                            x = slice(c * S, (c + 1) * S)
                            for w_, a in split3(WH[:, w], WL[:, w], XTH[:, x], XTL[:, x]):
                                last = mm(dst[:, g * S:(g + 1) * S], w_, a, start=n == 0, stop=n == 5)
                                n += 1
                    last.then_inc(done, 1)
                else:
                    pe.wait_ge(ql_ready, b + 1)
                    for kt in range(2):
                        n = 0
                        for c in range(2):
                            w = slice(W_V + c * D, W_V + (c + 1) * D)
                            x = slice(c * S + kt * HT, c * S + (kt + 1) * HT)
                            for a, w_ in split3(XTH[:, x], XTL[:, x], WH[:, w], WL[:, w]):
                                last = mm(WBK[1][0:HT, kt * D:(kt + 1) * D], a, w_, start=n == 0, stop=n == 5)
                                n += 1
                    last.then_inc(v_done, 1)

            def out_transpose(b):
                pe.wait_ge(on_ready, b + 1)
                pe.wait_ge(kl_ready, b + 1)
                for c in range(2):
                    for qt in range(2):
                        last = nc.tensor.transpose(WBK[0][:, c * S + qt * HT:c * S + (qt + 1) * HT],
                                                   ON[0:HT, qt * D + c * 128:qt * D + (c + 1) * 128], ident[0:HT, 0:HT])
                last.then_inc(ot_done, 1)

            def out_project(b):
                pe.wait_ge(otl_ready, b + 1)
                pe.wait_ge(v_ready, b + 1)
                for qt in range(2):
                    n = 0
                    for c in range(2):
                        w = slice(W_O + c * D, W_O + (c + 1) * D)
                        x = slice(c * S + qt * HT, c * S + (qt + 1) * HT)
                        for a, w_ in split3(OTH[:, x], OTL[:, x], WH[:, w], WL[:, w]):
                            last = mm(WBK[1][0:HT, qt * D:(qt + 1) * D], a, w_, start=n == 0, stop=n == 5)
                            n += 1
                last.then_inc(y_done, 1)

            def batch(b, par, first, last_):
                n = b * NH
                for s in range(STEPS):
                    if s < NH:
                        g, hh = s // 8, s % 8
                        if s == 0:
                            pe.wait_ge(qm_ready, b + 1)
                            pe.wait_ge(kl_ready, b + 1)
                        pe.wait_ge(scaled, n + s + 1)
                        k = slice(g * S, (g + 1) * S)
                        for qt in range(2):
                            q = slice(s * S + qt * HT, s * S + (qt + 1) * HT)
                            for i, (a, k_) in enumerate(split3(QMH[par][:, q], QML[par][:, q], KH[par][:, k], KL[par][:, k])):
                                last = mm(SBK[s % 2][0:HT, qt * S:(qt + 1) * S], a, k_, start=i == 0, stop=i == 2)
                        last.then_inc(s_done, 1)
                    if not first:
                        if s == 1:
                            out_transpose(b - 1)
                        if s == 3:
                            out_project(b - 1)
                    if not last_:
                        for at, stage in ((5, "x"), (7, "q"), (9, "k"), (11, "v")):
                            if s == at:
                                project(b + 1, 1 - par, stage, first)
                    h = s - 2
                    if 0 <= h < NH:
                        pe.wait_ge(exp_done, n + h + 3)
                        pe.wait_ge(pt_ready[h % 2], 8 * b + h // 2 + 1)
                        for kt in range(2):
                            for qt in range(2):
                                last = nc.tensor.transpose(TBK[h % 2][0:HT, kt * S + qt * HT:kt * S + (qt + 1) * HT],
                                                           P[h % 2][0:HT, qt * S + kt * HT:qt * S + (kt + 1) * HT], ident[0:HT, 0:HT])
                        last.then_inc(transposed, 1)
                    h = s - 3
                    if 0 <= h < NH:
                        if h == 0:
                            if not first:
                                pe.wait_ge(on_ready, b)
                            pe.wait_ge(v_ready, b + 1)
                        pe.wait_ge(pt_ready[h % 2], 8 * b + h // 2 + 2)
                        for qt in range(2):
                            for kt in range(2):
                                v = V[par][0:HT, (kt * NH + h) * (HD + 1):(kt * NH + h + 1) * (HD + 1)]
                                last = mm(OBK[qt][0:HT, h * (HD + 1):(h + 1) * (HD + 1)],
                                          PT[h % 2][0:HT, kt * S + qt * HT:kt * S + (qt + 1) * HT], v, start=kt == 0, stop=kt == 1)
                        last.then_inc(pv_done, 1)

            for stage in "xqkv":
                project(0, 0, stage, True)
            batches(pe, batch)
            out_transpose(B - 1)
            out_project(B - 1)
            meet(pe)
            def logits(b, j, par):
                pe.wait_ge(rtl_ready, b + 3)
                hold(pe)
                for qt in range(2):
                    at = bass.ds(b * S + qt * HT, HT)
                    n = 0
                    for c in range(2):
                        w = slice(W_GATE + c * E, W_GATE + (c + 1) * E)
                        for a, w_ in split3(TOKH[:, c, at], TOKL[:, c, at], WH[:, w], WL[:, w]):
                            last = mm(bank[2 + par][0:HT, (2 * j + qt) * E:(2 * j + qt + 1) * E], a, w_, start=n == 0, stop=n == 5)
                            n += 1
                return last

            def group(g, par):
                for j in range(GROUP + 1):
                    if j < GROUP:
                        b = GROUP * g + j
                        pe.wait_ge(row_ready, b + 1)
                        pe.wait_ge(rtl_ready, b + 1)
                        for c in range(2):
                            for qt in range(2):
                                last = nc.tensor.transpose(WBK[j % 2][:, c * S + qt * HT:c * S + (qt + 1) * HT],
                                                           ROWS3[par][0:HT, 2 * j + qt, c * 128:(c + 1) * 128], ident[0:HT, 0:HT])
                        last.then_inc(rt_done, 1)
                    if j > 0:
                        last = logits(GROUP * g + j - 1, j - 1, par)
                last.then_inc(lg_done, 1)
                pe.wait_ge(score_ready, g + 1)
                for t in range(2 * GROUP):
                    last = nc.tensor.transpose(bank[6 + t // 4][0:E, (t % 4) * HT:(t % 4 + 1) * HT], ROWS3[par][0:HT, t, D:ROW], ident[0:HT, 0:HT])
                last.then_inc(sct_done, 1)
            pairs(pe, GB, group)
            meet(pe)
            def down(k, par):
                for i in range(2):
                    if i == 0:
                        pe.wait_ge(hl_ready, 4 * k + 6)
                    pe.wait_ge(sh_added, 2 * k + i + 1)
                    for u in range(2):
                        n = 0
                        for c in range(4):
                            w = slice(W_SD + c * D, W_SD + (c + 1) * D)
                            x = slice(c * CHUNK + (2 * i + u) * HT, c * CHUNK + (2 * i + u + 1) * HT)
                            for a, w_ in split3(SHH[par][:, x], SHL[par][:, x], WH[:, w], WL[:, w]):
                                last = mm(bank[4 + i][0:HT, u * D:(u + 1) * D], a, w_, start=n == 0, stop=n == 11)
                                n += 1
                    last.then_inc(down_done, 1)

            def chunk(k, par):
                for m in range(4):
                    pe.wait_ge(hf_ready, 4 * k + m + 1)
                    hold(pe)
                    for i, w0 in enumerate((W_SG, W_SU)):
                        n = 0
                        for c in range(2):
                            w = slice(w0 + c * SF + m * 128, w0 + c * SF + (m + 1) * 128)
                            for w_, a in split3(WH[:, w], WL[:, w], TOKH[:, c, token_columns(k)], TOKL[:, c, token_columns(k)]):
                                last = mm(bank[2 * (m % 2) + i][:, 0:CHUNK], w_, a, start=n == 0, stop=n == 5)
                                n += 1
                    last.then_inc(gu_done, 1)
                    if m % 2 == 0:
                        pe.wait_ge(count_ready, 2 * k + m // 2 + 1)
                        mm(bank[7][:, 0:1], C[:, C_ONES:C_ONES + 128], COUNT, start=True, stop=True).then_inc(total_done, 1)
                down(k, par)
            pairs(pe, KS, chunk)
            meet(pe)
            pe.wait_ge(slots, 2)
            mm(bank[0][:, 0:1], C[:, C_ONES:C_ONES + 128], CGT, start=True, stop=True)
            mm(bank[1][:, 0:1], C[:, C_LOW:C_LOW + 128], CEQ, start=True, stop=True).then_inc(gt_total, 1)
            pe.wait_ge(slots, 9)
            mm(bank[2][:, 0:1], C[:, C_LOW:C_LOW + 128], LASTC, start=True, stop=True).then_inc(offs_done, 1)
            pe.wait_ge(slots, 12)
            for j in range(NJ):
                last = nc.tensor.transpose(bank[4 + j // 4][0:HT, (j % 4) * 128:(j % 4 + 1) * 128], RANK[:, j * HT:(j + 1) * HT], ident)
            last.then_inc(slot_t_done, 1)
            for q in range(E // QE):
                par = q % 2
                pe.wait_ge(hot_ready, q + 1)
                bo = BO[par][0:HT, :].rearrange("p (b w) -> p b w", b=SLOT_B)
                ao = AO[par][0:HT, :].rearrange("p (ha w) -> p ha w", ha=2 * SLOT_A)
                for ei in range(QE):
                    e = QE * q + ei
                    n = 0
                    for j in range(NJ):
                        for c in range(8):
                            col = j * 8 * QE + ei * 8 + c
                            last = mm(bank[e // 8][0:SLOT_B, (e % 8) * 2 * SLOT_A:(e % 8 + 1) * 2 * SLOT_A],
                                      bo[:, :, col], ao[:, :, col], start=n == 0, stop=n == 63)
                            n += 1
                last.then_inc(hot_used, 1)
            pe.drain().then_inc(idx_done, 2)
            meet(pe)
            def token_transposes(e, par):
                pe.wait_ge(xg_in[par], 48 * e + 96 - 48 * par)
                pe.wait_ge(xg_set, 2)
                for i in range(4):
                    c, m0, tiles = i % 2, 4 * (i // 2), (4, 2)[i // 2]
                    pe.wait_ge(xgl_ready, 4 * e + i + 1)
                    for m in range(m0, m0 + tiles):
                        n = slot_rows(m)
                        last = nc.tensor.transpose(bank[6 + c][:, (m - m0) * 128:(m - m0) * 128 + n],
                                                   XG[par][0:n, m * ROW + c * 128:m * ROW + (c + 1) * 128], ident[0:n, 0:n])
                    last.then_inc(xgt_done, 1)

            def expert(e, par, first, last_):
                pe.wait_ge(xgl_ready, 4 * e + 6)
                for i in range(2):
                    pe.wait_ge(wl_ready[i], e + 1)
                for n_ in range(2):
                    for m in range(8):
                        s = 8 * n_ + m
                        pe.wait_ge(ehf_ready, 16 * e + s + 1)
                        for i in range(2):
                            n = 0
                            for c in range(2):
                                w = slice(i * 2048 + c * FF + m * 128, i * 2048 + c * FF + (m + 1) * 128)
                                x = slice(c * CAP + n_ * CHUNK, c * CAP + (n_ + 1) * CHUNK)
                                for w_, a in split3(WEH[par][:, w], WEL[par][:, w], XGH[:, x], XGL[:, x]):
                                    last = mm(bank[2 * (s % 2) + i][:, 0:CHUNK], w_, a, start=n == 0, stop=n == 5)
                                    n += 1
                        last.then_inc(egu_done, 1)
                if not last_:
                    token_transposes(e + 1, 1 - par)
                pe.wait_ge(ehl_ready, 16 * e + 18)
                pe.wait_ge(wl_ready[2], e + 1)
                for m in range(SLOT_TILES):
                    rows = slot_rows(m)
                    pe.wait_ge(eo_ready, 6 * e + m + 1)
                    n = 0
                    for k in range(8):
                        x = slice(k * CAP + m * 128, k * CAP + m * 128 + rows)
                        w = slice(2 * 2048 + k * D, 2 * 2048 + (k + 1) * D)
                        for a, w_ in split3(HEH[:, x], HEL[:, x], WEH[par][:, w], WEL[par][:, w]):
                            last = mm(bank[4 + m % 2][0:rows, 0:D], a, w_, start=n == 0, stop=n == 23)
                            n += 1
                    last.then_inc(edown_done, 1)

            token_transposes(0, 0)
            experts_loop(pe, expert)
            meet(pe)


def constants():
    c = np.zeros((128, C_ALL), np.float32)
    p = np.arange(128)
    c[:, C_ID:C_ID + 128] = np.eye(128)
    c[:, C_ONES:C_ONES + 128] = p[:, None] // 8 == p[None] // 8
    c[:, C_LOW:C_LOW + 128] = (p[:, None] // 8 == p[None] // 8) & (p[:, None] < p[None])
    pos = np.arange(S)
    for qt in range(2):
        q = qt * HT + np.arange(HT)
        decay = np.exp(-0.01 * np.abs(q[:, None] - pos[None])) / 16 / WSCALE ** 2
        c[:HT, C_DECAY + qt * S:C_DECAY + (qt + 1) * S] = decay
    c[:, C_MASK:C_MASK + 8] = p[:, None] // 16 == np.arange(8)[None]
    tok = np.arange(8)[None, None] * CH + np.arange(NJ)[None, :, None] * HT + p[:, None, None]
    tok = tok.reshape(128, 64)
    c[:, C_TOK:C_TOK + 64] = tok // 128 * 128
    c[:, C_TOK + 64:C_TOK + 128] = tok % 128
    c[:, C_BIT:C_BIT + 32] = 2.0 ** np.maximum(29 - np.arange(32), 0)
    c[:, C_EPS] = EPS
    c[:, C_IOTA:C_IOTA + 32] = np.arange(32)
    return c


def kernel(x, L0_tok_conv_w, L0_tok_conv_b, L0_tok_ln_gamma, L0_tok_ln_beta, L0_attn_W_q, L0_attn_W_k, L0_attn_W_v,
           L0_attn_W_o, L0_attn_W_down_kv, L0_attn_W_up_k, L0_attn_W_up_v, L0_ffn_gate_w, L0_ffn_Wg, L0_ffn_Wu,
           L0_ffn_Wd, L0_ffn_Sg, L0_ffn_Su, L0_ffn_Sd):
    import concourse.bacc as bacc
    from concourse.bass_utils import run_bass_kernel_spmd

    a = np.asarray
    xp = np.pad(a(x), ((0, 0), (0, 1), (0, 0))).reshape(B, S, 4, 128).transpose(0, 3, 2, 1).reshape(B, 128, 4 * S)

    def experts(w, n):
        w = a(w)
        return w.reshape(E, w.shape[1], n, 128).transpose(0, 3, 2, 1).reshape(E, 128, n * w.shape[1])

    data = {
        "x_t": xp, "conv_w": a(L0_tok_conv_w).transpose(2, 1, 0).reshape(2 * D, D), "conv_b": L0_tok_conv_b,
        "gamma": L0_tok_ln_gamma, "beta": L0_tok_ln_beta, "wq": L0_attn_W_q, "wk_t": a(L0_attn_W_k).T,
        "wv_t": a(L0_attn_W_v).T, "wo": L0_attn_W_o, "w_down": L0_attn_W_down_kv, "w_up_k": L0_attn_W_up_k,
        "w_up_v": L0_attn_W_up_v, "gate": a(L0_ffn_gate_w).T, "s_g": a(L0_ffn_Sg).T, "s_u": a(L0_ffn_Su).T,
        "s_d": a(L0_ffn_Sd).T, "e_g": experts(L0_ffn_Wg, 2), "e_u": experts(L0_ffn_Wu, 2),
        "e_d": experts(L0_ffn_Wd, 8), "const": constants(),
    }
    nc = bacc.Bacc("TRN2", target_bir_lowering=False, num_devices=1)
    data = {k: np.ascontiguousarray(a(v)) for k, v in data.items()}
    args = {k: nc.dram_tensor(k, v.shape, mybir.dt.from_np(v.dtype), kind="ExternalInput").ap() for k, v in data.items()}
    out = nc.dram_tensor("out", (T, D), F32, kind="ExternalOutput").ap()
    build(nc, **args, out=out)
    r = run_bass_kernel_spmd(nc, [data], core_ids=[0])
    return r.results[0]["out"].reshape(B, S, D)
```

```python
import numpy as np
import concourse.bass as bass
from concourse import mybir
from contextlib import ExitStack

F32, F16, I32 = mybir.dt.float32, mybir.dt.float16, mybir.dt.int32
ALU = mybir.AluOpType
ACT = mybir.ActivationFunctionType
AX = mybir.AxisListType

B, S, D = 32, 188, 256
HT = S // 2
TILES = 2 * B
T = B * S
NH, HD = 16, 16
E, CAP = 16, 2 * T // 16
FF, SF = 4 * D, 2 * D
DL = 64
ROW = D + E
WSCALE = 64.0
HSCALE = 4.0
EPS = 1e-5
RING = 4
CH = T // 8
NJ = CH // HT
SLOT_A, SLOT_B = 24, 32
SLOT_TILES = 6
GROUP = 4
CHUNK = 2 * S

C_ID, C_ONES, C_LOW, C_DECAY = 0, 128, 256, 384
C_MASK = C_DECAY + 2 * S
C_TOK = C_MASK + 1
C_BIT = C_TOK + 64
C_EPS = C_BIT + 32
C_ROW = C_EPS + 1
C_ALL = C_ROW + 1

W_CONV, W_Q, W_K, W_V, W_O = 0, 1024, 2048, 3072, 3584
W_GATE = 4608
W_SG = W_GATE + 2 * E
W_SU, W_SD = W_SG + 2 * SF, W_SG + 4 * SF
W_ALL = W_SD + 4 * D


class Chain:

    def __init__(self, eng, sem):
        self.eng, self.sem, self.base, self.n = eng, sem, 0, 0

    def link(self, ins):
        self.mark(ins)
        self.wait()

    def mark(self, ins):
        ins.then_inc(self.sem, 1)
        self.n += 1

    def wait(self):
        self.eng.wait_ge(self.sem, self.base + self.n)

    def enter(self, i, per):
        self.start, self.per, self.n = self.base + self.n, per, 0
        self.base = self.start + i * per

    def leave(self, trips):
        assert self.n == self.per, (self.n, self.per)
        self.base, self.n = self.start + trips * self.per, 0


def build(nc, x_t, conv_w, conv_b, gamma, beta, wq, wk_t, wv_t, wo, w_down, w_up_k, w_up_v, gate, s_g, s_u, s_d,
          e_g, e_u, e_d, const, out):
    xtab = nc.dram_tensor("token_table", (T, ROW), F32)
    sctab = nc.dram_tensor("score_table", (E, T), F32)
    ctx = ExitStack()
    with ctx:
        def sb(name, shape, dt=F32):
            return ctx.enter_context(nc.sbuf_tensor(name, shape, dt))

        def sem(name):
            return ctx.enter_context(nc.semaphore(name))

        bank = [ctx.enter_context(nc.psum_tensor(f"bank{i}", [128, 512], F32)) for i in range(8)]

        C = sb("constants", [128, C_ALL])
        ident = C[:, C_ID:C_ID + 128]
        H = sb("hidden", [128, TILES, D])
        MV = sb("mean_var", [128, TILES, 2])
        RSTD = sb("rstd", [128, TILES, 1])
        WH = sb("weights_hi", [128, W_ALL], F16)
        WL = sb("weights_lo", [128, W_ALL], F16)
        ARENA = sb("arena", [128, 25000])

        class Place:
            def __init__(self, at=0):
                self.at = at

            def __call__(self, cols, dt=F32):
                words = cols if dt in (F32, I32) else (cols + 1) // 2
                v = ARENA[:, self.at:self.at + words]
                self.at += words
                assert self.at <= 25000, self.at
                return v if dt == F32 else v.bitcast(dt)

        at0 = Place()
        WS = at0(W_ALL)
        WKT, WVT = at0(512), at0(512)
        WDN, WUK, WUV = at0(128), at0(512), at0(256)
        M1 = at0(256)
        BIAS, GAM, BET = at0(D), at0(D), at0(D)
        XS = [at0(4 * S) for _ in range(2)]
        XH = [at0(4 * S, F16) for _ in range(2)]
        XL = [at0(4 * S, F16) for _ in range(2)]
        STAT, STATN = [at0(6) for _ in range(2)], [at0(6) for _ in range(2)]
        AGGR, MVB = at0(4).rearrange("p (t n) -> p t n", t=2), [at0(4).rearrange("p (t n) -> p t n", t=2) for _ in range(2)]
        SDB, NMR = [at0(2) for _ in range(2)], [at0(2) for _ in range(2)]
        LN = [at0(D) for _ in range(4)]
        SD = at0(TILES)
        at2 = Place()
        XN = at2(2 * D)
        XTH, XTL = (at2(2 * S, F16) for _ in range(2))
        QH = at2(4 * S, F16)
        QX = [at2(4 * S, F16) for _ in range(2)]
        KH = [at2(4 * S, F16) for _ in range(2)]
        KL = [at2(4 * S, F16) for _ in range(2)]
        V = [at2(2 * NH * 32) for _ in range(2)]
        SC = [at2(2 * S) for _ in range(RING)]
        P = [at2(2 * S) for _ in range(RING)]
        PT = [at2(2 * S) for _ in range(RING)]
        MAX, NEG = at2(2 * NH), at2(2 * NH)
        SUMS = [at2(2 * NH) for _ in range(2)]
        RS = at2(2 * NH * 32)
        OS, ON = at2(4 * S), at2(4 * S)
        OH, OX = at2(4 * S, F16), at2(4 * S, F16)
        AGGR2 = at2(4)
        STAT2 = [at2(6) for _ in range(2)]

        at3 = Place()
        XTOK = {"hi": at3(2 * T, F16), "lo": at3(2 * T, F16)}
        TOKH, TOKL = (v.rearrange("p (c n) -> p c n", c=2) for v in XTOK.values())
        at4 = Place(at3.at)
        ROWS = [at3(2 * GROUP * ROW) for _ in range(2)]
        LMAX, LSUM, LINV = at3(8), at3(8), at3(8)
        LEXP = at3(8 * E)
        SD2 = at3(TILES)
        SCT = [at3(2 * GROUP * HT) for _ in range(2)]
        SC8 = at4(CH)
        HIT = at4(CH)
        BITI, THR, CAND, GAIN, COUNT = at4(32, I32), at4(1, I32), at4(1, I32), at4(1, I32), at4(1)
        search_end = at4.at
        SGEL, SHF = [at4(CHUNK) for _ in range(2)], [at4(CHUNK) for _ in range(RING)]
        SHH = [at4(4 * CHUNK, F16) for _ in range(2)]
        SHL = [at4(4 * CHUNK, F16) for _ in range(2)]
        SOUT = [at4(4 * D) for _ in range(2)]
        at5 = Place()
        QE = 4
        QC = QE * 64
        BO = [at5(SLOT_B * QC, F16) for _ in range(2)]
        assert at5.at <= at4.at
        at5 = Place(search_end)
        ONE, EQ, RANK = at5(CH), at5(CH), at5(CH)
        CGT, CEQ, NEED, LASTC, OFF = at5(1), at5(1), at5(1), at5(1), at5(1)
        SLI, SAI = at5(8 * 128, I32), at5(8 * 128, I32)
        A16, B16, TH16 = (at5(8 * 128, F16) for _ in range(3))
        I32T, ILOW = at5(E * SLOT_A), at5(E * SLOT_A)
        HW = H[:, :, :].rearrange("p t n -> p (t n)")
        AO = [HW[:, i * 24 * QC:(i + 1) * 24 * QC].bitcast(F16) for i in range(2)]
        IDX = sb("slot_tokens", [128, E, SLOT_TILES], I32)
        WEH = [HW[:, i * 3072:(i + 1) * 3072].bitcast(F16) for i in range(2)]
        WEL = [HW[:, 6144 + i * 3072:6144 + (i + 1) * 3072].bitcast(F16) for i in range(2)]
        EO = [HW[:, 12288 + i * 1536:12288 + (i + 1) * 1536] for i in range(2)]
        at6 = Place()
        WST = at6(3 * 2048)
        XG = [at6(SLOT_TILES * ROW) for _ in range(2)]
        XGH, XGL = at6(2 * CAP, F16), at6(2 * CAP, F16)
        HEH, HEL = at6(8 * CAP, F16), at6(8 * CAP, F16)
        EGEL, EHF = [at6(CHUNK) for _ in range(2)], [at6(CHUNK) for _ in range(RING)]
        IDXG, IDXS = [at6(SLOT_TILES, I32) for _ in range(2)], [at6(SLOT_TILES, I32) for _ in range(2)]
        WT = [at6(SLOT_TILES) for _ in range(2)]

        engines_met = sem("engines_met")
        block = ctx.enter_context(nc.Block())
        met = {}

        def meet(eng):
            eng.drain().then_inc(engines_met, 1)
            met[id(eng)] = met.get(id(eng), 0) + 5
            eng.wait_ge(engines_met, met[id(eng)])

        const_in, weights_in, fold_in = sem("const_in"), sem("weights_in"), sem("fold_in")
        summed, half_added = sem("kv_summed"), sem("half_added")
        m1_done, m1_copied, fold_done, fold_copied = sem("m1_done"), sem("m1_copied"), sem("fold_done"), sem("fold_copied")
        hi_done, lo_done = sem("w_hi_done"), sem("w_lo_done")
        x_in = [sem("x_in0"), sem("x_in1")]
        xh_ready, xl_ready = sem("xh_ready"), sem("xl_ready")
        conv_done, conv_free, dve1 = sem("conv_done"), sem("conv_free"), sem("dve1")
        sd_done, norm_done, gam_done, bet_done = (
            sem("sd_done"), sem("norm_done"), sem("gamma_done"), sem("beta_done"))
        stats_ready, inv_ready = sem("stats_ready"), sem("inv_ready")
        dve_ln, sd2_done, rstd_done = sem("dve_ln"), sem("sd2_done"), sem("rstd_done")

        def split3(hi_a, lo_a, hi_b, lo_b):
            return ((hi_a, hi_b), (lo_a, hi_b), (hi_a, lo_b))

        scaled, exp_done, transposed, pv_done = sem("scaled+2"), sem("exp_done+4"), sem("transposed+4"), sem("pv_done+4")
        s_done = sem("scores_done")
        pt_ready = [sem("pt_even+1"), sem("pt_odd+1")]
        neg_ready, dve2 = sem("neg_ready"), sem("dve2")
        os_ready, rs_ready, rt_done2, on_ready, oh_ready, ox_ready, y_done, y_added = (
            sem(n) for n in ("os_ready", "rs_ready", "rs_turned", "on_ready", "oh_ready", "ox_ready", "y_done", "y_added"))
        xn_ready, xt_done, xth_ready, xtl_ready = (sem(n) for n in ("xn_ready", "xt_done", "xth_ready", "xtl_ready"))
        q_done, qh_ready, ql_ready = (sem(n) for n in ("q_done", "qh_ready", "ql_ready"))
        k_done, kh_ready, kl_ready, v_done, v_ready = (
            sem(n) for n in ("k_done", "kh_ready", "kl_ready", "v_done", "v_ready"))
        SBK, TBK, WBK, OBK = bank[0:2], bank[2:4], bank[4:6], bank[6:8]
        T_LAG, V_LAG = 3, 5

        def behind(s, lag, first):
            back, h = (1, s - lag + NH) if s < lag else (0, s - lag)
            return None if first and back else (back, h)

        def batches(eng, body):
            body(0, 0, True, False)
            with eng.Fori(0, B // 2 - 1) as i:
                body(2 * i + 1, 1, False, False)
                body(2 * i + 2, 0, False, False)
            body(B - 1, 1, False, True)

        def conv_batches(eng, body):
            body(0, 0, 0)
            body(1, 1, 1)
            with eng.Fori(1, B // 2 - 1) as i:
                body(2 * i, 0, 2)
                body(2 * i + 1, 1, 2)
            body(B - 2, 0, 2)
            body(B - 1, 1, 2)

        def hsplit(ap):
            return ap.rearrange("p (t n) -> p t n", t=2)

        row_ready, rt_done, rth_ready, rtl_ready = sem("row_ready"), sem("rt_done"), sem("rth_ready"), sem("rtl_ready+2")
        lg_done, lmax_done, lsub_done, lexp_done = sem("lg_done"), sem("lmax_done"), sem("lsub_done"), sem("lexp_done")
        lsum_done, score_ready, sct_done, sct_ready = sem("lsum_done"), sem("score_ready"), sem("sct_done"), sem("sct_ready")
        rstd2_in, rstd2_done = sem("sd_of_h1"), sem("rstd_of_h1")
        table_out = [sem("table_out0+32"), sem("table_out1+32")]
        sc8_in, gu_done, gel_ready, hf_ready, hh_ready, hl_ready = (
            sem(n) for n in ("sc8_in", "gu_done", "gel_ready", "hf_ready+2", "hh_ready", "hl_ready+4"))
        down_done, sh_added = sem("down_done"), sem("sh_added+2")
        sh_out = [sem("sh_out0+16"), sem("sh_out1+16")]
        search, count_ready, total_done = sem("search"), sem("count_ready"), sem("total_done")
        slots, gt_total, offs_done, slot_t_done, hot_ready, hot_used, hot_a, hot_row = (
            sem(n) for n in ("slots", "gt_total", "offs_done", "slot_t_done", "hot_ready", "hot_used", "hot_a", "hot_row"))
        idx_done, ones_ready = sem("idx_done"), sem("ones_ready")
        w_in = [sem(f"w_in{i}") for i in range(3)]
        wh_ready = [sem(f"wh_ready{i}") for i in range(3)]
        wl_ready = [sem(f"wl_ready{i}") for i in range(3)]
        idx_ready, xg_in, xg_set = sem("idx_ready"), [sem("xg_in0"), sem("xg_in1")], sem("xg_set")
        xgt_done, xgh_ready, xgl_ready = sem("xgt_done"), sem("xgh_ready"), sem("xgl_ready+2")
        egu_done, egel_ready, ehf_ready, ehh_ready, ehl_ready = (
            sem(n) for n in ("egu_done", "egel_ready", "ehf_ready+2", "ehh_ready", "ehl_ready+4"))
        edown_done, eo_ready, scattered, wt_ready = sem("edown_done"), sem("eo_ready+2"), sem("scattered"), sem("wt_ready")
        ROWS3 = [v.rearrange("p (t n) -> p t n", n=ROW) for v in ROWS]
        GB = 8
        KS = T // CHUNK

        def pairs(eng, n, body):
            with eng.Fori(0, n // 2) as i:
                body(2 * i, 0)
                body(2 * i + 1, 1)

        def experts_loop(eng, body):
            body(0, 0, True, False)
            with eng.Fori(0, E // 2 - 1) as i:
                body(2 * i + 1, 1, False, False)
                body(2 * i + 2, 0, False, False)
            body(E - 1, 1, False, True)

        def slot_rows(m):
            return 128 if m < SLOT_TILES - 1 else CAP - 128 * (SLOT_TILES - 1)

        down_bank = (4, 5, 0, 1, 2, 3)

        def token_columns(k):
            return bass.ts(k, CHUNK)

        passed = sem("waits_passed")

        def hold(eng):
            eng.sem_inc(passed, 1)

        @block.sync
        def _(sp):
            sp.dma_start(C[:, :], const).then_inc(const_in, 16)
            for dst, src in ((WKT, wk_t), (WVT, wv_t), (WDN, w_down)):
                sp.dma_start(dst.rearrange("p (c n) -> p c n", c=2), src.rearrange("(c p) n -> p c n", p=128)).then_inc(fold_in, 16)
            sp.dma_start(WUK[0:DL, :], w_up_k).then_inc(fold_in, 16)
            sp.dma_start(WUV[0:DL, :], w_up_v).then_inc(fold_in, 16)
            sp.dma_start(WS[:, W_CONV:W_Q].rearrange("p (c n) -> p c n", c=4), conv_w.rearrange("(c p) n -> p c n", p=128)).then_inc(weights_in, 16)
            for o, src, c in ((W_Q, wq, 2), (W_O, wo, 4)):
                sp.dma_start(WS[:, o:o + 1024].rearrange("p (c n) -> p c n", c=c), src.rearrange("(c p) n -> p c n", p=128)).then_inc(weights_in, 16)
            sp.dma_start(WS[:, W_GATE:W_SG].rearrange("p (c n) -> p c n", c=2), gate.rearrange("(c p) n -> p c n", p=128)).then_inc(weights_in, 16)
            for o, src, c in ((W_SG, s_g, 2), (W_SU, s_u, 2), (W_SD, s_d, 4)):
                sp.dma_start(WS[:, o:o + 1024].rearrange("p (c n) -> p c n", c=c), src.rearrange("(c p) n -> p c n", p=128)).then_inc(weights_in, 16)
            for dst, src in ((BIAS, conv_b), (GAM, gamma), (BET, beta)):
                sp.dma_start(dst, src.rearrange("(a n) -> a n", a=1).broadcast_to((128, D))).then_inc(weights_in, 16)
            sp.dma_start(XS[0], x_t[0, :, :]).then_inc(x_in[0], 16)
            sp.dma_start(XS[1], x_t[1, :, :]).then_inc(x_in[1], 16)
            with sp.Fori(1, B // 2) as i:
                for par in range(2):
                    sp.wait_ge(xl_ready, 2 * i + par - 1)
                    sp.dma_start(XS[par], x_t[2 * i + par, :, :]).then_inc(x_in[par], 16)
            meet(sp)
            meet(sp)
            def group(g, par):
                sp.wait_ge(score_ready, g + 1)
                hold(sp)
                sp.dma_start(xtab[bass.ts(g, 2 * GROUP * HT), :].rearrange("(t p) n -> p t n", p=HT), ROWS3[par][0:HT, :, :]).then_inc(table_out[par], 16)
                sp.wait_ge(sct_ready, g + 1)
                hold(sp)
                sp.dma_start(sctab[:, bass.ts(g, 2 * GROUP * HT)], SCT[par][0:E, :]).then_inc(table_out[par], 16)
            pairs(sp, GB, group)
            for par in range(2):
                sp.wait_ge(table_out[par], 32 * (GB // 2 + 1))
            meet(sp)
            sp.dma_start(SC8, sctab[:, :].rearrange("e (c n) -> (e c) n", c=8)).then_inc(sc8_in, 16)

            def chunk(k, par):
                sp.wait_ge(sh_added, 2 * k + 4)
                hold(sp)
                sp.dma_start(out[bass.ts(k, CHUNK), :].rearrange("(t p) n -> p t n", p=HT),
                             SOUT[par][0:HT, :].rearrange("p (t n) -> p t n", t=4)).then_inc(sh_out[par], 16)
            pairs(sp, KS, chunk)
            for par in range(2):
                sp.wait_ge(sh_out[par], 16 * (KS // 2 + 1))
            meet(sp)
            meet(sp)

            def load(e, i):
                src = (e_g, e_u, e_d)[i]
                sp.dma_start(WST[:, i * 2048:(i + 1) * 2048], src[e, :, :]).then_inc(w_in[i], 16)

            for i in range(3):
                load(0, i)
            with sp.Fori(1, E) as e:
                for i in range(3):
                    sp.wait_ge(wl_ready[i], 2 * e)
                    hold(sp)
                    load(e, i)
            meet(sp)

        @block.gpsimd
        def _(pool):
            def add_beta(b, par):
                for qt in range(2):
                    pool.wait_ge(gam_done, 2 * b + qt + 1)
                    nc.gpsimd.tensor_tensor(H[0:HT, bass.ds(2 * b + qt, 1), :].rearrange("p t n -> p (t n)"), LN[2 * par + qt][0:HT, :], BET[0:HT, :], ALU.add).then_inc(bet_done, 1)

            def low_input(b, par):
                pool.wait_ge(xh_ready, b + 1)
                nc.gpsimd.tensor_tensor(XL[par], XS[par], XH[par], ALU.subtract).then_inc(xl_ready, 1)

            def conv_batch(b, par, age):
                if not isinstance(b, int) or b < B - 1:
                    low_input(b + 1, 1 - par)
                if age >= 2:
                    add_beta(b - 2, par)

            low_input(0, 0)
            conv_batches(pool, conv_batch)
            add_beta(B - 2, 0)
            add_beta(B - 1, 1)
            meet(pool)

            def negate(b, par, first, last):
                for s in range(NH):
                    pool.wait_ge(scaled, NH * b + s + 3)
                    hold(pool)
                    nc.gpsimd.tensor_scalar(NEG[0:HT, s::NH], MAX[0:HT, s::NH], -1.0, None, ALU.mult).then_inc(neg_ready, 1)
            batches(pool, negate)
            meet(pool)
            meet(pool)

            def low_hidden(dst, f, hi, ready_in, count, ready):
                pool.wait_ge(ready_in, count)
                nc.gpsimd.tensor_tensor(dst, f, hi, ALU.subtract).then_inc(ready, 1)

            def chunk(k, par):
                for m in range(4):
                    c = slice(m * CHUNK, (m + 1) * CHUNK)
                    low_hidden(SHL[par][:, c], SHF[m], SHH[par][:, c], hh_ready, 4 * k + m + 1, hl_ready)
            pool.sem_inc(hl_ready, RING)
            pairs(pool, KS, chunk)
            meet(pool)
            nc.gpsimd.memset(ONE, 1.0).then_inc(ones_ready, 1)
            meet(pool)
            pool.sem_inc(ehl_ready, RING)
            for par in range(2):
                nc.gpsimd.memset(XG[par], 0.0).then_inc(xg_set, 1)
            pool.wait_ge(xg_set, 2)

            def list_slots(place, e, par, count):
                nc.gpsimd.tensor_copy(place[par], IDX[:, e, :]).then_inc(idx_ready, 1)
                pool.wait_ge(idx_ready, count)
                hold(pool)

            def gather(par, m):
                n = slot_rows(m)
                nc.gpsimd.indirect_dma_start(
                    XG[par][0:n, m * ROW:(m + 1) * ROW], None, xtab[:, :],
                    bass.IndirectOffsetOnAxis(ap=IDXG[par][0:n, m:m + 1], axis=0)).then_inc(xg_in[par], 16)

            def scatter(e, par, m):
                n = slot_rows(m)
                pool.wait_ge(eo_ready, 6 * e + m + 3)
                hold(pool)
                nc.gpsimd.indirect_dma_start(
                    out[:, :], bass.IndirectOffsetOnAxis(ap=IDXS[par][0:n, m:m + 1], axis=0),
                    EO[par][0:n, m * D:(m + 1) * D], None, compute_op=ALU.add).then_inc(scattered, 16)

            def expert(e, par, first, last):
                for n in range(2):
                    for m in range(8):
                        s = 8 * n + m
                        if not last:
                            if s == 0:
                                list_slots(IDXG, e + 1, 1 - par, 2 if first else 2 * e + 1)
                            if s < SLOT_TILES:
                                gather(1 - par, s)
                        if not first:
                            if s == SLOT_TILES:
                                list_slots(IDXS, e - 1, 1 - par, 2 * e + 1 + (not last))
                            if SLOT_TILES <= s < 2 * SLOT_TILES:
                                scatter(e - 1, 1 - par, s - SLOT_TILES)
                            if s == 15:
                                pool.wait_ge(scattered, 96 * e)
                        c = slice(m * CAP + n * CHUNK, m * CAP + (n + 1) * CHUNK)
                        low_hidden(HEL[:, c], EHF[s % RING], HEH[:, c], ehh_ready, 16 * e + s + 1, ehl_ready)

            list_slots(IDXG, 0, 0, 1)
            for m in range(SLOT_TILES):
                gather(0, m)
            experts_loop(pool, expert)
            list_slots(IDXS, E - 1, 1, 2 * E)
            for m in range(SLOT_TILES):
                scatter(E - 1, 1, m)
            pool.wait_ge(scattered, 96 * E)
            meet(pool)

        @block.scalar
        def _(act):
            def copy(dst, src, scale=1.0):
                return nc.scalar.activation(dst, src, ACT.Copy, scale=scale)

            act.sem_inc(exp_done, RING)
            act.sem_inc(pt_ready[0], 1)
            act.wait_ge(m1_done, 1)
            copy(M1[0:DL, :], bank[0][0:DL, 0:256]).then_inc(m1_copied, 1)
            for i in range(3):
                act.wait_ge(fold_done, i + 1)
                copy(WS[:, W_K + 512 * i:W_K + 512 * (i + 1)], bank[2 + i][:, :]).then_inc(fold_copied, 1)
            act.wait_ge(weights_in, 16 * 10)
            act.wait_ge(half_added, 4)
            act.wait_ge(fold_copied, 3)
            copy(WH[:, :], WS, WSCALE).then_inc(hi_done, 1)
            def normalize(b, par):
                act.wait_ge(inv_ready, b + 1)
                for qt in range(2):
                    last = nc.scalar.activation(LN[2 * par + qt][0:HT, :], H[0:HT, 2 * b + qt, :], ACT.Identity,
                                                scale=SDB[par][0:HT, qt:qt + 1], bias=NMR[par][0:HT, qt:qt + 1])
                last.then_inc(norm_done, 1)

            def high_input(b, par):
                act.wait_ge(x_in[par], 8 * b + 16 - 8 * par)
                act.wait_ge(conv_done, 2 * b + 2)
                copy(XH[par], XS[par]).then_inc(xh_ready, 1)

            def conv_batch(b, par, age):
                if not isinstance(b, int) or b < B - 2:
                    high_input(b + 2, par)
                if age >= 1:
                    normalize(b - 1, 1 - par)
                deviation(b, par)

            def deviation(b, par):
                act.wait_ge(stats_ready, b + 1)
                nc.scalar.activation(SDB[par][0:HT, :], MVB[par][0:HT, :, 1], ACT.Sqrt, bias=C[0:HT, C_EPS:C_EPS + 1]).then_inc(sd_done, 1)

            high_input(0, 0)
            high_input(1, 1)
            conv_batches(act, conv_batch)
            normalize(B - 1, 1)
            act.wait_ge(rstd_done, 1)
            nc.scalar.activation(SD[0:HT, :], MV[0:HT, :, 1], ACT.Sqrt, bias=C[0:HT, C_EPS:C_EPS + 1]).then_inc(sd2_done, 1)
            meet(act)

            def project_halves(b, par, stage):
                if stage == "x":
                    act.wait_ge(xt_done, b + 1)
                    copy(XTH, WBK[1][:, 0:2 * S]).then_inc(xth_ready, 1)
                elif stage[0] == "q":
                    i = int(stage[1])
                    act.wait_ge(q_done, 2 * b + i + 1)
                    copy(QH[:, i * 2 * S:(i + 1) * 2 * S], WBK[1 - i][:, 0:2 * S]).then_inc(qh_ready, 1)
                elif stage[0] == "k":
                    i = int(stage[1])
                    act.wait_ge(k_done, 2 * b + i + 1)
                    copy(KH[par][:, i * 2 * S:(i + 1) * 2 * S], WBK[1 - i][:, 0:2 * S]).then_inc(kh_ready, 1)
                else:
                    act.wait_ge(v_done, b + 1)
                    for kt in range(2):
                        src = WBK[1][0:HT, kt * D:(kt + 1) * D].rearrange("p (h d) -> p h d", d=HD)
                        dst = hsplit(V[par][0:HT, :])[:, kt, :].rearrange("p (h r d) -> p h r d", r=2, d=HD)
                        last = copy(dst, src.unsqueeze(2).broadcast_to((HT, NH, 2, HD)), 1.0 / WSCALE)
                    last.then_inc(v_ready, 1)

            def out_half(b, stage):
                if stage[0] == "s":
                    i = int(stage[1])
                    act.wait_ge(pv_done, NH * b + (i + 1) * NH // 2 + RING)
                    copy(OS[:, i * 2 * S:(i + 1) * 2 * S], OBK[i][:, 0:2 * S]).then_inc(os_ready, 1)
                else:
                    act.wait_ge(on_ready, 2 * b + 2)
                    copy(OH, ON).then_inc(oh_ready, 1)

            def evacuate(n, s, first):
                at = behind(s, T_LAG, first)
                if at and at[1] % 2 == 0:
                    act.wait_ge(transposed, n + s - T_LAG + RING + 1)
                    act.wait_ge(pv_done, n + s - T_LAG + 1)
                    copy(PT[at[1] % RING][0:HT, :], TBK[0][0:HT, 0:2 * S]).then_inc(pt_ready[0], 1)

            def batch(b, par, first, last):
                n = b * NH
                for s in range(NH):
                    if s == 1 and not first:
                        out_half(b - 1, "s0")
                    if s == V_LAG and not first:
                        out_half(b - 1, "s1")
                    if s == 6 and not first:
                        out_half(b - 1, "h")
                    if not last:
                        for at, stage in ((7, "x"), (10, "q0"), (11, "q1"), (13, "k0"), (14, "k1")):
                            if s == at:
                                project_halves(b + 1, 1 - par, stage)
                    evacuate(n, s, first)
                    act.wait_ge(neg_ready, n + s + 1)
                    act.wait_ge(transposed, n + s + 1)
                    for qt in range(2):
                        ins = nc.scalar.activation(P[s % RING][0:HT, qt * S:(qt + 1) * S], SC[s % RING][0:HT, qt * S:(qt + 1) * S],
                                                   ACT.Exp, bias=NEG[0:HT, qt * NH + s:qt * NH + s + 1],
                                                   accum_out=SUMS[par][0:HT, qt * NH + s:qt * NH + s + 1])
                    ins.then_inc(exp_done, 1)
                    if not last and s == NH - 1:
                        project_halves(b + 1, 1 - par, "v")

            for stage in ("x", "q0", "q1", "k0", "k1", "v"):
                project_halves(0, 0, stage)
            batches(act, batch)
            for s in range(T_LAG):
                evacuate(B * NH, s, False)
            for stage in ("s0", "s1", "h"):
                out_half(B - 1, stage)
            meet(act)

            nc.scalar.activation(SD2[0:HT, :], MV[0:HT, :, 1], ACT.Sqrt, bias=C[0:HT, C_EPS:C_EPS + 1]).then_inc(rstd2_in, 1)

            def group(g, par):
                for j in range(GROUP):
                    act.wait_ge(rt_done, GROUP * g + j + 1)
                    hold(act)
                    copy(TOKH[:, :, bass.ts(GROUP * g + j, S)], WBK[j % 2][:, 0:2 * S].rearrange("p (c n) -> p c n", c=2)).then_inc(rth_ready, 1)
                act.wait_ge(lsub_done, g + 1)
                nc.scalar.activation(LEXP[0:HT, :], LEXP[0:HT, :], ACT.Exp, scale=1.0 / WSCALE).then_inc(lexp_done, 1)
                act.wait_ge(sct_done, g + 1)
                act.wait_ge(table_out[par], 16 * g + 32 - 16 * par)
                for i in range(2):
                    last = copy(SCT[par][0:E, i * 376:(i + 1) * 376], bank[6 + i][0:E, 0:376])
                last.then_inc(sct_ready, 1)
            pairs(act, GB, group)
            meet(act)

            def chunk(k, par):
                for m in range(5):
                    if m < 4:
                        act.wait_ge(gu_done, 4 * k + m + 1)
                        act.wait_ge(hf_ready, 4 * k + m + 1)
                        nc.scalar.activation(SGEL[m % 2], bank[2 * (m % 2)][:, 0:CHUNK], ACT.Gelu, scale=1.0 / WSCALE).then_inc(gel_ready, 1)
                    if m > 0:
                        act.wait_ge(hf_ready, 4 * k + m + 2)
                        copy(SHH[par][:, (m - 1) * CHUNK:m * CHUNK], SHF[m - 1]).then_inc(hh_ready, 1)
            pairs(act, KS, chunk)
            meet(act)
            for q in range(E // QE):
                rows = AO[q % 2][0:HT, SLOT_A * QC:2 * SLOT_A * QC]
                act.wait_ge(hot_ready, q + 1)
                copy(rows, rows, C[0:HT, C_ROW:C_ROW + 1]).then_inc(hot_row, 1)
            meet(act)

            def high_weights(e, i, h, par):
                act.wait_ge(w_in[i], 16 * e + 16)
                c = slice((2 * i + h) * 1024, (2 * i + h + 1) * 1024)
                copy(WEH[par][:, c], WST[:, c], WSCALE).then_inc(wh_ready[i], 1)

            def high_tokens(e):
                for i in range(4):
                    act.wait_ge(xgt_done, 4 * e + i + 1)
                    c, t0, n = i % 2, 512 * (i // 2), (512, CAP - 512)[i // 2]
                    copy(XGH[:, c * CAP + t0:c * CAP + t0 + n], bank[6 + c][:, 0:n]).then_inc(xgh_ready, 1)

            def expert(e, par, first, last):
                for s in range(17):
                    if s < 16:
                        act.wait_ge(egu_done, 16 * e + s + 1)
                        act.wait_ge(ehf_ready, 16 * e + s + 1)
                        nc.scalar.activation(EGEL[s % 2], bank[2 * (s % 2)][:, 0:CHUNK], ACT.Gelu, scale=1.0 / WSCALE).then_inc(egel_ready, 1)
                    if s > 0:
                        n, m = (s - 1) // 8, (s - 1) % 8
                        act.wait_ge(ehf_ready, 16 * e + s + 2)
                        copy(HEH[:, m * CAP + n * CHUNK:m * CAP + (n + 1) * CHUNK], EHF[(s - 1) % RING]).then_inc(ehh_ready, 1)
                    if s in (2, 3, 6, 7, 10, 11) and not last:
                        high_weights(e + 1, s // 4, s % 2, 1 - par)
                if not last:
                    high_tokens(e + 1)

            for i in range(3):
                for h in range(2):
                    high_weights(0, i, h, 0)
            high_tokens(0)
            experts_loop(act, expert)
            meet(act)

        @block.vector
        def _(dve):
            for s_, v_ in ((conv_free, 2), (scaled, 2), (pt_ready[1], 1)):
                dve.sem_inc(s_, v_)
            dve.wait_ge(fold_in, 16 * 5)
            nc.vector.tensor_tensor(WKT, WKT, WVT, ALU.add).then_inc(summed, 1)
            dve.wait_ge(weights_in, 16 * 10)
            dve.wait_ge(const_in, 16)
            for c in range(4):
                half = WS[:, W_CONV + 256 * c + 128 * (c % 2):W_CONV + 256 * c + 128 * (c % 2) + 128]
                nc.vector.scalar_tensor_tensor(half, ident, 0.5, half, ALU.mult, ALU.add).then_inc(half_added, 1)
            dve.wait_ge(hi_done, 1)
            nc.vector.scalar_tensor_tensor(WL[:, :], WS, WSCALE, WH[:, :], ALU.mult, ALU.subtract).then_inc(lo_done, 1)

            conv_chain = Chain(dve, dve1)
            ln_chain = Chain(dve, dve_ln)

            def gather_stats(chain, stat, b):
                hold(dve)
                for qt in range(2):
                    chain.mark(nc.vector.bn_stats(stat[qt][0:HT, :], H[0:HT, 2 * b + qt, :]))

            def aggregate(chain, stat, keep):
                chain.wait()
                hold(dve)
                for qt in range(2):
                    chain.mark(nc.vector.bn_aggr(keep[0:HT, qt, :], stat[qt][0:HT, :]))

            def of_normal(b):
                dve.wait_ge(bet_done, 2 * b + 2)
                gather_stats(ln_chain, STATN, b)

            def keep_mean(b):
                ln_chain.mark(nc.vector.tensor_copy(MV[0:HT, bass.ts(b, 2), :] if not isinstance(b, int) else MV[0:HT, 2 * b:2 * b + 2, :], AGGR[0:HT, :, :]))

            def inverse(b, par):
                dve.wait_ge(sd_done, b + 1)
                ln_chain.link(nc.vector.reciprocal(SDB[par][0:HT, :], SDB[par][0:HT, :]))
                nc.vector.scalar_tensor_tensor(NMR[par][0:HT, :], MVB[par][0:HT, :, 0], -1.0, SDB[par][0:HT, :],
                                               ALU.mult, ALU.mult).then_inc(inv_ready, 1)

            def times_gamma(b, par):
                dve.wait_ge(norm_done, b + 1)
                for qt in range(2):
                    nc.vector.tensor_tensor(LN[2 * par + qt][0:HT, :], LN[2 * par + qt][0:HT, :], GAM[0:HT, :], ALU.mult).then_inc(gam_done, 1)

            def conv_batch(b, par, age):
                for qt in range(2):
                    dve.wait_ge(conv_done, 2 * b + qt + 5)
                    conv_chain.mark(nc.vector.scalar_tensor_tensor(
                        H[0:HT, 2 * b + qt, :], bank[2 * par + qt][0:HT, 0:D], 1.0 / WSCALE, BIAS[0:HT, :], ALU.mult, ALU.add))
                if age >= 1:
                    inverse(b - 1, 1 - par)
                conv_chain.wait()
                dve.sem_inc(conv_free, 1)
                gather_stats(conv_chain, STAT, b)
                aggregate(conv_chain, STAT, MVB[par])
                if age >= 2:
                    of_normal(b - 2)
                conv_chain.wait()
                dve.sem_inc(stats_ready, 1)
                if age >= 2:
                    aggregate(ln_chain, STATN, AGGR)
                    ln_chain.wait()
                    keep_mean(b - 2)
                if age >= 1:
                    times_gamma(b - 1, 1 - par)

            conv_batch(0, 0, 0)
            conv_batch(1, 1, 1)
            with dve.Fori(0, B // 2 - 1) as i:
                conv_chain.enter(i, 12)
                ln_chain.enter(i, 12)
                conv_batch(2 * i + 2, 0, 2)
                conv_batch(2 * i + 3, 1, 2)
            conv_chain.leave(B // 2 - 1)
            ln_chain.leave(B // 2 - 1)
            inverse(B - 1, 1)
            times_gamma(B - 1, 1)
            for b in (B - 2, B - 1):
                of_normal(b)
                aggregate(ln_chain, STATN, AGGR)
                ln_chain.wait()
                keep_mean(b)
                ln_chain.wait()
            dve.sem_inc(rstd_done, 1)
            dve.wait_ge(sd2_done, 1)
            nc.vector.reciprocal(RSTD[0:HT, :, 0], SD[0:HT, :]).then_inc(rstd_done, 1)
            meet(dve)
            def x_norm(b):
                for qt in range(2):
                    t = 2 * b + qt
                    last = nc.vector.tensor_scalar(XN[0:HT, qt * D:(qt + 1) * D], H[0:HT, t, :], MV[0:HT, t, 0:1],
                                                   RSTD[0:HT, t, :], ALU.subtract, ALU.mult)
                last.then_inc(xn_ready, 1)

            def low(dst, src, hi, hi_ready, count, ready):
                dve.wait_ge(hi_ready, count)
                nc.vector.tensor_tensor(dst, src, hi, ALU.subtract).then_inc(ready, 1)

            def project_halves(b, par, stage):
                if stage == "n":
                    x_norm(b)
                elif stage == "x":
                    low(XTL, WBK[1][:, 0:2 * S], XTH, xth_ready, b + 1, xtl_ready)
                elif stage[0] == "q":
                    i = int(stage[1])
                    c = slice(i * 2 * S, (i + 1) * 2 * S)
                    dve.wait_ge(qh_ready, 2 * b + i + 1)
                    nc.vector.scalar_tensor_tensor(QX[par][:, c], QH[:, c], C[:, C_MASK:C_MASK + 1], WBK[1 - i][:, 0:2 * S],
                                                   ALU.mult, ALU.add).then_inc(ql_ready, 1)
                else:
                    i = int(stage[1])
                    c = slice(i * 2 * S, (i + 1) * 2 * S)
                    low(KL[par][:, c], WBK[1 - i][:, 0:2 * S], KH[par][:, c], kh_ready, 2 * b + i + 1, kl_ready)

            def out_half(b, par, stage):
                if stage == "r":
                    dve.wait_ge(exp_done, NH * (b + 1) + RING)
                    nc.vector.reciprocal(SUMS[par][0:HT, :], SUMS[par][0:HT, :]).then_inc(inv_done, 1)
                    dve.wait_ge(inv_done, b + 1)
                    nc.vector.tensor_copy(RS[0:HT, :].rearrange("p (n r) -> p n r", r=32),
                                          SUMS[par][0:HT, :].unsqueeze(2).broadcast_to((HT, 2 * NH, 32))).then_inc(rs_ready, 1)
                elif stage[0] == "n":
                    i = int(stage[1])
                    dve.wait_ge(os_ready, 2 * b + i + 1)
                    dve.wait_ge(rt_done2, 2 * b + i + 1)
                    c = slice(i * 2 * S, (i + 1) * 2 * S)
                    nc.vector.tensor_tensor(ON[:, c], OS[:, c], WBK[1 - i][:, 0:2 * S], ALU.mult).then_inc(on_ready, 1)
                else:
                    dve.wait_ge(oh_ready, b + 1)
                    nc.vector.scalar_tensor_tensor(OX, OH, C[:, C_MASK:C_MASK + 1], ON, ALU.mult, ALU.add).then_inc(ox_ready, 1)

            def add_out(b):
                dve.wait_ge(y_done, b + 1)
                both = H[0:HT, bass.ts(b, 2), :].rearrange("p t n -> p (t n)")
                nc.vector.scalar_tensor_tensor(both, WBK[0][0:HT, 0:2 * D], 1.0 / WSCALE, both, ALU.mult, ALU.add).then_inc(y_added, 1)
                dve.wait_ge(y_added, b + 1)
                hold(dve)
                for qt in range(2):
                    nc.vector.bn_stats(STAT2[qt][0:HT, :], H[0:HT, 2 * b + qt, :]).then_inc(dve2, 1)
                dve.wait_ge(dve2, 5 * b + 2)
                hold(dve)
                for qt in range(2):
                    nc.vector.bn_aggr(AGGR2[0:HT, 2 * qt:2 * qt + 2], STAT2[qt][0:HT, :]).then_inc(dve2, 1)
                dve.wait_ge(dve2, 5 * b + 4)
                nc.vector.tensor_copy(MV[0:HT, bass.ts(b, 2), :], hsplit(AGGR2[0:HT, :])).then_inc(dve2, 1)

            inv_done = sem("inv_done")

            def evacuate(n, s, first):
                at = behind(s, T_LAG, first)
                if at and at[1] % 2 == 1:
                    dve.wait_ge(transposed, n + s - T_LAG + RING + 1)
                    dve.wait_ge(pv_done, n + s - T_LAG + 1)
                    nc.vector.tensor_copy(PT[at[1] % RING][0:HT, :], TBK[1][0:HT, 0:2 * S]).then_inc(pt_ready[1], 1)

            def batch(b, par, first, last):
                n = b * NH
                for s in range(NH):
                    dve.wait_ge(s_done, n + s + 1)
                    dve.wait_ge(exp_done, n + s + 1)
                    hold(dve)
                    for qt in range(2):
                        last_half = nc.vector.tensor_tensor_reduce(
                            out=SC[s % RING][0:HT, qt * S:(qt + 1) * S], in0=SBK[s % 2][0:HT, qt * S:(qt + 1) * S],
                            in1=C[0:HT, C_DECAY + qt * S:C_DECAY + (qt + 1) * S], scale=1.0, scalar=-3e38,
                            op0=ALU.mult, op1=ALU.max, accum_out=MAX[0:HT, qt * NH + s:qt * NH + s + 1])
                    last_half.then_inc(scaled, 1)
                    evacuate(n, s, first)
                    if not first:
                        for at, stage in ((1, "r"), (4, "n0"), (5, "n1"), (7, "x")):
                            if s == at:
                                out_half(b - 1, 1 - par, stage)
                        if s == 9:
                            add_out(b - 1)
                    if not last:
                        for at, stage in ((3, "n"), (7, "x"), (10, "q0"), (11, "q1"), (13, "k0"), (14, "k1")):
                            if s == at:
                                project_halves(b + 1, 1 - par, stage)

            for stage in ("n", "x", "q0", "q1", "k0", "k1"):
                project_halves(0, 0, stage)
            batches(dve, batch)
            for s in range(T_LAG):
                evacuate(B * NH, s, False)
            for stage in ("r", "n0", "n1", "x"):
                out_half(B - 1, 1, stage)
            add_out(B - 1)
            meet(dve)
            dve.sem_inc(rtl_ready, 2)
            for par in range(2):
                dve.sem_inc(table_out[par], 32)
            dve.wait_ge(rstd2_in, 1)
            nc.vector.reciprocal(RSTD[0:HT, :, 0], SD2[0:HT, :]).then_inc(rstd2_done, 1)
            dve.wait_ge(rstd2_done, 1)

            def group(g, par):
                dve.wait_ge(table_out[par], 16 * g + 32 - 16 * par)
                hold(dve)
                for j in range(GROUP):
                    for qt in range(2):
                        t = 2 * GROUP * g + 2 * j + qt
                        last = nc.vector.tensor_scalar(ROWS3[par][0:HT, 2 * j + qt, 0:D], H[0:HT, t, :], MV[0:HT, t, 0:1],
                                                       RSTD[0:HT, t, :], ALU.subtract, ALU.mult)
                    last.then_inc(row_ready, 1)
                for j in range(GROUP):
                    dve.wait_ge(rth_ready, GROUP * g + j + 1)
                    at = bass.ts(GROUP * g + j, S)
                    nc.vector.tensor_tensor(TOKL[:, :, at], WBK[j % 2][:, 0:2 * S].rearrange("p (c n) -> p c n", c=2),
                                            TOKH[:, :, at], ALU.subtract).then_inc(rtl_ready, 1)
                dve.wait_ge(lg_done, g + 1)
                logits = bank[2 + par][0:HT, 0:8 * E].rearrange("p (t n) -> p t n", n=E)
                exps = LEXP[0:HT, :].rearrange("p (t n) -> p t n", n=E)

                def spread(v):
                    return v[0:HT, :].unsqueeze(2).broadcast_to((HT, 8, E))
                nc.vector.tensor_reduce(LMAX[0:HT, :], logits, AX.X, ALU.max).then_inc(lmax_done, 1)
                dve.wait_ge(lmax_done, g + 1)
                nc.vector.tensor_tensor(exps, logits, spread(LMAX), ALU.subtract).then_inc(lsub_done, 1)
                dve.wait_ge(lexp_done, g + 1)
                nc.vector.tensor_reduce(LSUM[0:HT, :], exps, AX.X, ALU.add).then_inc(lsum_done, 1)
                dve.wait_ge(lsum_done, 2 * g + 1)
                nc.vector.reciprocal(LINV[0:HT, :], LSUM[0:HT, :]).then_inc(lsum_done, 1)
                dve.wait_ge(lsum_done, 2 * g + 2)
                nc.vector.tensor_tensor(ROWS3[par][0:HT, :, D:ROW], exps, spread(LINV), ALU.mult).then_inc(score_ready, 1)
            pairs(dve, GB, group)
            meet(dve)
            dve.sem_inc(hf_ready, 2)
            dve.sem_inc(sh_added, 2)
            for par in range(2):
                dve.sem_inc(sh_out[par], 16)
            find = Chain(dve, search)
            find.mark(nc.vector.tensor_copy(BITI, C[:, C_BIT:C_BIT + 32]))
            find.link(nc.vector.memset(THR, 0))
            dve.wait_ge(sc8_in, 16)

            def count(it):
                find.link(nc.vector.tensor_tensor(CAND, THR, BITI[:, bass.ds(it, 1)], ALU.bitwise_or))
                nc.vector.tensor_scalar(HIT, SC8, CAND.bitcast(F32), None, ALU.is_ge, ALU.add, accum_out=COUNT).then_inc(count_ready, 1)

            def decide(it):
                dve.wait_ge(total_done, it + 1)
                find.link(nc.vector.tensor_scalar(GAIN, bank[7][:, 0:1], float(CAP), C[:, bass.ds(C_BIT + it, 1)], ALU.is_ge, ALU.mult))
                find.link(nc.vector.tensor_tensor(THR, THR, GAIN, ALU.bitwise_or))

            def down_out(k, par, i):
                dve.wait_ge(down_done, 2 * k + i + 1)
                if i == 0:
                    dve.wait_ge(sh_out[par], 8 * k + 16 - 8 * par)
                nc.vector.scalar_tensor_tensor(
                    SOUT[par][0:HT, i * 2 * D:(i + 1) * 2 * D], bank[4 + i][0:HT, :], 1.0 / (WSCALE * HSCALE),
                    H[0:HT, bass.ts(2 * k + i, 2), :].rearrange("p t n -> p (t n)"), ALU.mult, ALU.add).then_inc(sh_added, 1)

            def chunk(k, par, first):
                for m in range(4):
                    if m % 2 == 0:
                        count(2 * k + m // 2)
                    dve.wait_ge(gel_ready, 4 * k + m + 1)
                    dve.wait_ge(hl_ready, 4 * k + m + 1)
                    nc.vector.scalar_tensor_tensor(SHF[m], bank[2 * (m % 2) + 1][:, 0:CHUNK], HSCALE / WSCALE, SGEL[m % 2],
                                                   ALU.mult, ALU.mult).then_inc(hf_ready, 1)
                    if m % 2 == 1:
                        decide(2 * k + m // 2)
                    if m >= 2 and not first:
                        down_out(k - 1, 1 - par, m - 2)

            chunk(0, 0, True)
            with dve.Fori(0, KS // 2 - 1) as i2:
                find.enter(i2, 12)
                chunk(2 * i2 + 1, 1, False)
                chunk(2 * i2 + 2, 0, False)
            find.leave(KS // 2 - 1)
            chunk(KS - 1, 1, False)
            for i in range(2):
                down_out(KS - 1, 1, i)
            meet(dve)
            step = Chain(dve, slots)
            thr = THR.bitcast(F32)
            nc.vector.tensor_scalar(HIT, SC8, thr, None, ALU.is_gt, ALU.add, accum_out=CGT).then_inc(slots, 1)
            step.n += 1
            step.link(nc.vector.tensor_scalar(EQ, SC8, thr, None, ALU.is_equal, ALU.add, accum_out=CEQ))
            dve.wait_ge(ones_ready, 1)
            step.mark(nc.vector.tensor_tensor_scan(RANK, ONE, EQ, 0.0, ALU.mult, ALU.add))
            dve.wait_ge(gt_total, 1)
            step.link(nc.vector.tensor_scalar(NEED, bank[0][:, 0:1], -1.0, float(CAP), ALU.mult, ALU.add))
            step.link(nc.vector.tensor_tensor(NEED, NEED, bank[1][:, 0:1], ALU.subtract))
            step.link(nc.vector.scalar_tensor_tensor(EQ, RANK, NEED, EQ, ALU.is_le, ALU.mult))
            step.link(nc.vector.tensor_tensor(HIT, HIT, EQ, ALU.add))
            step.link(nc.vector.tensor_tensor_scan(RANK, ONE, HIT, 0.0, ALU.mult, ALU.add))
            step.link(nc.vector.tensor_copy(LASTC, RANK[:, CH - 1:CH]))
            dve.wait_ge(offs_done, 1)
            step.link(nc.vector.tensor_copy(OFF, bank[2][:, 0:1]))
            step.link(nc.vector.scalar_tensor_tensor(RANK, RANK, OFF, HIT, ALU.add, ALU.mult))
            step.link(nc.vector.tensor_scalar(RANK, RANK, -1.0, None, ALU.add))
            dve.wait_ge(slot_t_done, 1)
            for i in range(2):
                step.mark(nc.vector.tensor_copy(SLI[0:HT, i * 512:(i + 1) * 512], bank[4 + i][0:HT, :]))
            step.wait()
            step.mark(nc.vector.tensor_scalar(SAI[0:HT, :], SLI[0:HT, :], 5, None, ALU.arith_shift_right))
            step.link(nc.vector.tensor_scalar(SLI[0:HT, :], SLI[0:HT, :], 31, None, ALU.bitwise_and))
            step.mark(nc.vector.tensor_copy(A16[0:HT, :], SAI[0:HT, :]))
            step.mark(nc.vector.tensor_copy(B16[0:HT, :], SLI[0:HT, :]))
            tok = C[0:HT, C_TOK:C_TOK + 64].rearrange("p (j c) -> p j c", c=8)
            step.mark(nc.vector.tensor_copy(TH16[0:HT, :].rearrange("p (j e c) -> p j e c", e=E, c=8),
                                            tok.unsqueeze(2).broadcast_to((HT, NJ, E, 8))))
            step.wait()

            def quarter(v, q):
                return v[0:HT, :].rearrange("p (j w) -> p j w", j=NJ)[:, :, q * 8 * QE:(q + 1) * 8 * QE]

            for q in range(E // QE):
                par = q % 2
                if q >= 2:
                    dve.wait_ge(hot_used, q - 1)
                bo = BO[par][0:HT, :].rearrange("p (b j w) -> p b j w", b=SLOT_B, j=NJ)
                ao = AO[par][0:HT, :].rearrange("p (h a j w) -> p h a j w", h=2, a=SLOT_A, j=NJ)
                for b_ in range(SLOT_B):
                    last = nc.vector.tensor_scalar(bo[:, b_], quarter(B16, q), float(b_), None, ALU.is_equal)
                for a_ in range(SLOT_A):
                    last = nc.vector.tensor_scalar(ao[:, 1, a_], quarter(A16, q), float(a_), None, ALU.is_equal)
                last.then_inc(hot_a, 1)
                dve.wait_ge(hot_a, q + 1)
                nc.vector.tensor_tensor(ao[:, 0], ao[:, 1], quarter(TH16, q).unsqueeze(1).broadcast_to((HT, SLOT_A, NJ, 8 * QE)),
                                        ALU.mult).then_inc(hot_ready, 1)
            dve.wait_ge(idx_done, 2)
            for i in range(2):
                src = bank[i][0:SLOT_B, 0:8 * 2 * SLOT_A].rearrange("p (e h a) -> p e h a", e=8, h=2)
                low_ = ILOW[0:SLOT_B, i * 192:(i + 1) * 192].rearrange("p (e a) -> p e a", e=8)
                step.link(nc.vector.tensor_copy(low_, src[:, :, 1]))
                step.link(nc.vector.scalar_tensor_tensor(I32T[0:SLOT_B, i * 192:(i + 1) * 192].rearrange("p (e a) -> p e a", e=8), src[:, :, 0], float(HT), low_, ALU.mult, ALU.add))
            for i in range(4):
                src = I32T[0:SLOT_B, :].rearrange("p (e m i) -> p e m i", e=E, i=4)
                step.mark(nc.vector.tensor_copy(IDX[32 * i:32 * i + 32, :, :], src[:, :, :, i]))
            meet(dve)
            dve.sem_inc(xgl_ready, 2)
            dve.sem_inc(ehf_ready, 2)
            dve.sem_inc(eo_ready, 2)

            def low_weights(e, i, h, par):
                dve.wait_ge(wh_ready[i], 2 * e + h + 1)
                c = slice((2 * i + h) * 1024, (2 * i + h + 1) * 1024)
                nc.vector.scalar_tensor_tensor(WEL[par][:, c], WST[:, c], WSCALE, WEH[par][:, c],
                                               ALU.mult, ALU.subtract).then_inc(wl_ready[i], 1)

            def low_tokens(e, par, steps):
                for i in steps:
                    dve.wait_ge(xgh_ready, 4 * e + i + 1)
                    c, t0, n = i % 2, 512 * (i // 2), (512, CAP - 512)[i // 2]
                    w = slice(c * CAP + t0, c * CAP + t0 + n)
                    nc.vector.tensor_tensor(XGL[:, w], bank[6 + c][:, 0:n], XGH[:, w], ALU.subtract).then_inc(xgl_ready, 1)
                if 3 not in steps:
                    return
                rows = XG[par].rearrange("p (m n) -> p m n", n=ROW)[:, :, bass.ds(D + e, 1)]
                nc.vector.tensor_scalar(WT[par].unsqueeze(2), rows, 1.0 / (WSCALE * HSCALE), None, ALU.mult).then_inc(wt_ready, 1)

            def expert(e, par, first, last):
                for s in range(16):
                    dve.wait_ge(egel_ready, 16 * e + s + 1)
                    dve.wait_ge(ehl_ready, 16 * e + s + 1)
                    nc.vector.scalar_tensor_tensor(EHF[s % RING], bank[2 * (s % 2) + 1][:, 0:CHUNK], HSCALE / WSCALE, EGEL[s % 2],
                                                   ALU.mult, ALU.mult).then_inc(ehf_ready, 1)
                    if s in (4, 5, 8, 9, 12, 13) and not last:
                        low_weights(e + 1, s // 4 - 1, s % 2, 1 - par)
                if not last:
                    low_tokens(e + 1, 1 - par, (0, 1))
                dve.wait_ge(wt_ready, e + 1)
                for m in range(SLOT_TILES):
                    n = slot_rows(m)
                    dve.wait_ge(edown_done, 6 * e + m + 1)
                    nc.vector.tensor_scalar(EO[par][0:n, m * D:(m + 1) * D], bank[down_bank[m]][0:n, 0:D], WT[par][0:n, m:m + 1],
                                            None, ALU.mult).then_inc(eo_ready, 1)
                    if m == 1 and not last:
                        low_tokens(e + 1, 1 - par, (2, 3))

            for i in range(3):
                for h in range(2):
                    low_weights(0, i, h, 0)
            low_tokens(0, 0, range(4))
            experts_loop(dve, expert)
            meet(dve)

        @block.tensor
        def _(pe):
            mm = nc.tensor.matmul
            for s_, v_ in ((conv_done, 4), (transposed, RING), (pv_done, RING)):
                pe.sem_inc(s_, v_)
            pe.wait_ge(summed, 1)
            for c in range(2):
                last = mm(bank[0][0:DL, 0:256], WDN[:, c * DL:(c + 1) * DL], WKT[:, c * 256:(c + 1) * 256], start=c == 0, stop=c == 1)
            last.then_inc(m1_done, 1)
            pe.wait_ge(m1_copied, 1)
            for c in range(2):
                mm(bank[2 + c][:, :], M1[0:DL, c * 128:(c + 1) * 128], WUK[0:DL, :], start=True, stop=True).then_inc(fold_done, 1)
            for c in range(2):
                last = mm(bank[4][:, c * 256:(c + 1) * 256], M1[0:DL, c * 128:(c + 1) * 128], WUV[0:DL, :], start=True, stop=True)
            last.then_inc(fold_done, 1)
            pe.wait_ge(lo_done, 1)
            with pe.Fori(0, B // 2) as i:
                for par in range(2):
                    pe.wait_ge(xl_ready, 2 * i + par + 1)
                    pe.wait_ge(conv_free, 2 * i + par + 1)
                    for qt in range(2):
                        n = 0
                        for c in range(4):
                            w = slice(W_CONV + c * D, W_CONV + (c + 1) * D)
                            x = slice(c * S + qt * HT, c * S + (qt + 1) * HT)
                            for a, w_ in split3(XH[par][:, x], XL[par][:, x], WH[:, w], WL[:, w]):
                                last = mm(bank[2 * par + qt][0:HT, 0:D], a, w_, start=n == 0, stop=n == 11)
                                n += 1
                        last.then_inc(conv_done, 1)
            meet(pe)
            def project(b, par, stage, first):
                if stage == "x":
                    pe.wait_ge(xn_ready, b + 1)
                    if not first:
                        pe.wait_ge(on_ready, 2 * b - 3)
                    for c in range(2):
                        for qt in range(2):
                            last = nc.tensor.transpose(WBK[1][:, c * S + qt * HT:c * S + (qt + 1) * HT],
                                                       XN[0:HT, qt * D + c * 128:qt * D + (c + 1) * 128], ident[0:HT, 0:HT])
                    last.then_inc(xt_done, 1)
                elif stage[0] in "qk":
                    if stage == "q0":
                        pe.wait_ge(xtl_ready, b + 1)
                    if stage == "q1":
                        if not first:
                            pe.wait_ge(y_added, b - 1)
                    w0, done, read = (W_Q, q_done, None) if stage[0] == "q" else (W_K, k_done, ql_ready)
                    for g in (0, 1) if stage[1] == "0" else (2, 3):
                        if read is not None and g % 2 == 0:
                            pe.wait_ge(read, 2 * b + g // 2 + 1)
                        n = 0
                        for c in range(2):
                            w = slice(w0 + c * 2 * D + g * 128, w0 + c * 2 * D + (g + 1) * 128)
                            x = slice(c * S, (c + 1) * S)
                            for w_, a in split3(WH[:, w], WL[:, w], XTH[:, x], XTL[:, x]):
                                last = mm(WBK[1 - g // 2][:, (g % 2) * S:(g % 2 + 1) * S], w_, a, start=n == 0, stop=n == 5)
                                n += 1
                        if g % 2 == 1:
                            last.then_inc(done, 1)
                else:
                    if stage == "v0":
                        pe.wait_ge(kl_ready, 2 * b + 1)
                    for kt in (int(stage[1]),):
                        n = 0
                        for c in range(2):
                            w = slice(W_V + c * D, W_V + (c + 1) * D)
                            x = slice(c * S + kt * HT, c * S + (kt + 1) * HT)
                            for a, w_ in split3(XTH[:, x], XTL[:, x], WH[:, w], WL[:, w]):
                                last = mm(WBK[1][0:HT, kt * D:(kt + 1) * D], a, w_, start=n == 0, stop=n == 5)
                                n += 1
                    if stage == "v1":
                        last.then_inc(v_done, 1)

            def out_turn(b):
                pe.wait_ge(rs_ready, b + 1)
                pe.wait_ge(v_ready, b + 1)
                for g in range(4):
                    for qt in range(2):
                        last = nc.tensor.transpose(WBK[1 - g // 2][:, (g % 2) * S + qt * HT:(g % 2) * S + (qt + 1) * HT],
                                                   RS[0:HT, (qt * NH + 4 * g) * 32:(qt * NH + 4 * g + 4) * 32], ident[0:HT, 0:HT])
                    if g % 2 == 1:
                        last.then_inc(rt_done2, 1)

            def out_project(b):
                pe.wait_ge(ox_ready, b + 1)
                for qt in range(2):
                    for g in range(4):
                        w = slice(W_O + g * D, W_O + (g + 1) * D)
                        x = slice(g * S + qt * HT, g * S + (qt + 1) * HT)
                        for i, w_ in enumerate((WH[:, w], WL[:, w])):
                            last = mm(WBK[0][0:HT, qt * D:(qt + 1) * D], OX[:, x], w_, start=g + i == 0, stop=g + i == 4)
                last.then_inc(y_done, 1)

            def turn(b, n, s, first):
                at = behind(s, T_LAG, first)
                if at:
                    back, h = at
                    pe.wait_ge(exp_done, n + s - T_LAG + RING + 1)
                    pe.wait_ge(pt_ready[h % 2], 8 * (b - back) + h // 2 + 1)
                    for kt in range(2):
                        for qt in range(2):
                            last = nc.tensor.transpose(TBK[h % 2][0:HT, kt * S + qt * HT:kt * S + (qt + 1) * HT],
                                                       P[h % RING][0:HT, qt * S + kt * HT:qt * S + (kt + 1) * HT], ident[0:HT, 0:HT])
                    last.then_inc(transposed, 1)

            def weigh(b, par, n, s, first):
                at = behind(s, V_LAG, first)
                if at:
                    back, h = at
                    if h % 8 == 0 and not back and not first:
                        pe.wait_ge(os_ready, 2 * b - 1 + h // 8)
                    if h == 0:
                        pe.wait_ge(v_ready, b + 1)
                    pe.wait_ge(pt_ready[h % 2], 8 * (b - back) + h // 2 + 2)
                    g, j = h // 4, 32 * (h % 4)
                    for kt in range(2):
                        v = V[(par + back) % 2][0:HT, (kt * NH + h) * 32:(kt * NH + h + 1) * 32]
                        last = mm(OBK[g // 2][j:j + 32, (g % 2) * S:(g % 2 + 1) * S], v, PT[h % RING][0:HT, kt * S:(kt + 1) * S],
                                  start=kt == 0, stop=kt == 1)
                    last.then_inc(pv_done, 1)

            def batch(b, par, first, last_):
                n = b * NH
                for s in range(NH):
                    if s == 0:
                        pe.wait_ge(ql_ready, 2 * b + 2)
                        pe.wait_ge(kl_ready, 2 * b + 2)
                    pe.wait_ge(scaled, n + s + 1)
                    g, j = s // 4, 32 * (s % 4)
                    k = slice(g * S, (g + 1) * S)
                    for qt in range(2):
                        q = slice(g * S + qt * HT, g * S + (qt + 1) * HT)
                        for i, k_ in enumerate((KH[par], KL[par])):
                            last = mm(SBK[s % 2][0:HT, qt * S:(qt + 1) * S], QX[par][j:j + 32, q], k_[j:j + 32, k], start=i == 0, stop=i == 1)
                    last.then_inc(s_done, 1)
                    turn(b, n, s, first)
                    weigh(b, par, n, s, first)
                    if not first:
                        if s == 3:
                            out_turn(b - 1)
                        if s == 8:
                            out_project(b - 1)
                    if not last_:
                        for at, stage in ((6, "x"), (9, "q0"), (10, "q1"), (12, "k0"), (13, "k1"), (14, "v0"), (15, "v1")):
                            if s == at:
                                project(b + 1, 1 - par, stage, first)

            for stage in ("x", "q0", "q1", "k0", "k1", "v0", "v1"):
                project(0, 0, stage, True)
            batches(pe, batch)
            for s in range(V_LAG):
                if s < T_LAG:
                    turn(B, B * NH, s, False)
                weigh(B, 0, B * NH, s, False)
            out_turn(B - 1)
            out_project(B - 1)
            meet(pe)
            def logits(b, j, par):
                pe.wait_ge(rtl_ready, b + 3)
                hold(pe)
                for qt in range(2):
                    at = bass.ds(b * S + qt * HT, HT)
                    n = 0
                    for c in range(2):
                        w = slice(W_GATE + c * E, W_GATE + (c + 1) * E)
                        for a, w_ in split3(TOKH[:, c, at], TOKL[:, c, at], WH[:, w], WL[:, w]):
                            last = mm(bank[2 + par][0:HT, (2 * j + qt) * E:(2 * j + qt + 1) * E], a, w_, start=n == 0, stop=n == 5)
                            n += 1
                return last

            def group(g, par):
                for j in range(GROUP + 1):
                    if j < GROUP:
                        b = GROUP * g + j
                        pe.wait_ge(row_ready, b + 1)
                        pe.wait_ge(rtl_ready, b + 1)
                        for c in range(2):
                            for qt in range(2):
                                last = nc.tensor.transpose(WBK[j % 2][:, c * S + qt * HT:c * S + (qt + 1) * HT],
                                                           ROWS3[par][0:HT, 2 * j + qt, c * 128:(c + 1) * 128], ident[0:HT, 0:HT])
                        last.then_inc(rt_done, 1)
                    if j > 0:
                        last = logits(GROUP * g + j - 1, j - 1, par)
                last.then_inc(lg_done, 1)
                pe.wait_ge(score_ready, g + 1)
                for t in range(2 * GROUP):
                    last = nc.tensor.transpose(bank[6 + t // 4][0:E, (t % 4) * HT:(t % 4 + 1) * HT], ROWS3[par][0:HT, t, D:ROW], ident[0:HT, 0:HT])
                last.then_inc(sct_done, 1)
            pairs(pe, GB, group)
            meet(pe)
            def down(k, par):
                for i in range(2):
                    if i == 0:
                        pe.wait_ge(hl_ready, 4 * k + 4 + RING)
                    pe.wait_ge(sh_added, 2 * k + i + 1)
                    for u in range(2):
                        n = 0
                        for c in range(4):
                            w = slice(W_SD + c * D, W_SD + (c + 1) * D)
                            x = slice(c * CHUNK + (2 * i + u) * HT, c * CHUNK + (2 * i + u + 1) * HT)
                            for a, w_ in split3(SHH[par][:, x], SHL[par][:, x], WH[:, w], WL[:, w]):
                                last = mm(bank[4 + i][0:HT, u * D:(u + 1) * D], a, w_, start=n == 0, stop=n == 11)
                                n += 1
                    last.then_inc(down_done, 1)

            def chunk(k, par, first):
                for m in range(4):
                    pe.wait_ge(hf_ready, 4 * k + m + 1)
                    hold(pe)
                    for i, w0 in enumerate((W_SG, W_SU)):
                        n = 0
                        for c in range(2):
                            w = slice(w0 + c * SF + m * 128, w0 + c * SF + (m + 1) * 128)
                            for w_, a in split3(WH[:, w], WL[:, w], TOKH[:, c, token_columns(k)], TOKL[:, c, token_columns(k)]):
                                last = mm(bank[2 * (m % 2) + i][:, 0:CHUNK], w_, a, start=n == 0, stop=n == 5)
                                n += 1
                    last.then_inc(gu_done, 1)
                    if m % 2 == 1:
                        pe.wait_ge(count_ready, 2 * k + m // 2 + 1)
                        mm(bank[7][:, 0:1], C[:, C_ONES:C_ONES + 128], COUNT, start=True, stop=True).then_inc(total_done, 1)
                    if m == 1 and not first:
                        down(k - 1, 1 - par)

            def chunk_pairs(eng, body):
                body(0, 0, True)
                with eng.Fori(0, KS // 2 - 1) as i:
                    body(2 * i + 1, 1, False)
                    body(2 * i + 2, 0, False)
                body(KS - 1, 1, False)
            chunk_pairs(pe, chunk)
            down(KS - 1, 1)
            meet(pe)
            pe.wait_ge(slots, 2)
            mm(bank[0][:, 0:1], C[:, C_ONES:C_ONES + 128], CGT, start=True, stop=True)
            mm(bank[1][:, 0:1], C[:, C_LOW:C_LOW + 128], CEQ, start=True, stop=True).then_inc(gt_total, 1)
            pe.wait_ge(slots, 9)
            mm(bank[2][:, 0:1], C[:, C_LOW:C_LOW + 128], LASTC, start=True, stop=True).then_inc(offs_done, 1)
            pe.wait_ge(slots, 12)
            for j in range(NJ):
                last = nc.tensor.transpose(bank[4 + j // 4][0:HT, (j % 4) * 128:(j % 4 + 1) * 128], RANK[:, j * HT:(j + 1) * HT], ident)
            last.then_inc(slot_t_done, 1)
            for q in range(E // QE):
                par = q % 2
                pe.wait_ge(hot_row, q + 1)
                bo = BO[par][0:HT, :].rearrange("p (b w) -> p b w", b=SLOT_B)
                ao = AO[par][0:HT, :].rearrange("p (ha w) -> p ha w", ha=2 * SLOT_A)
                for ei in range(QE):
                    e = QE * q + ei
                    n = 0
                    for j in range(NJ):
                        for c in range(8):
                            col = j * 8 * QE + ei * 8 + c
                            last = mm(bank[e // 8][0:SLOT_B, (e % 8) * 2 * SLOT_A:(e % 8 + 1) * 2 * SLOT_A],
                                      bo[:, :, col], ao[:, :, col], start=n == 0, stop=n == 63)
                            n += 1
                last.then_inc(hot_used, 1)
            pe.drain().then_inc(idx_done, 2)
            meet(pe)
            def token_transposes(e, par, steps):
                if 0 in steps:
                    pe.wait_ge(xg_in[par], 48 * e + 96 - 48 * par)
                    pe.wait_ge(xg_set, 2)
                for i in steps:
                    c, m0, tiles = i % 2, 4 * (i // 2), (4, 2)[i // 2]
                    pe.wait_ge(xgl_ready, 4 * e + i + 1)
                    for m in range(m0, m0 + tiles):
                        n = slot_rows(m)
                        last = nc.tensor.transpose(bank[6 + c][:, (m - m0) * 128:(m - m0) * 128 + n],
                                                   XG[par][0:n, m * ROW + c * 128:m * ROW + (c + 1) * 128], ident[0:n, 0:n])
                    last.then_inc(xgt_done, 1)

            def expert(e, par, first, last_):
                pe.wait_ge(xgl_ready, 4 * e + 6)
                for i in range(2):
                    pe.wait_ge(wl_ready[i], 2 * e + 2)
                for n_ in range(2):
                    for m in range(8):
                        s = 8 * n_ + m
                        pe.wait_ge(ehf_ready, 16 * e + s + 1)
                        if s < 2 and not first:
                            pe.wait_ge(eo_ready, 6 * e + 2 * s)
                        for i in range(2):
                            n = 0
                            for c in range(2):
                                w = slice(i * 2048 + c * FF + m * 128, i * 2048 + c * FF + (m + 1) * 128)
                                x = slice(c * CAP + n_ * CHUNK, c * CAP + (n_ + 1) * CHUNK)
                                for w_, a in split3(WEH[par][:, w], WEL[par][:, w], XGH[:, x], XGL[:, x]):
                                    last = mm(bank[2 * (s % 2) + i][:, 0:CHUNK], w_, a, start=n == 0, stop=n == 5)
                                    n += 1
                        last.then_inc(egu_done, 1)
                if not last_:
                    token_transposes(e + 1, 1 - par, (0, 1))
                pe.wait_ge(wl_ready[2], 2 * e + 2)
                for m in range(SLOT_TILES):
                    rows = slot_rows(m)
                    if m == 0:
                        pe.wait_ge(ehl_ready, 16 * e + 8 + RING)
                    if m == 2:
                        pe.wait_ge(ehl_ready, 16 * e + 16 + RING)
                    n = 0
                    for k in range(8):
                        x = slice(k * CAP + m * 128, k * CAP + m * 128 + rows)
                        w = slice(2 * 2048 + k * D, 2 * 2048 + (k + 1) * D)
                        for a, w_ in split3(HEH[:, x], HEL[:, x], WEH[par][:, w], WEL[par][:, w]):
                            last = mm(bank[down_bank[m]][0:rows, 0:D], a, w_, start=n == 0, stop=n == 23)
                            n += 1
                    last.then_inc(edown_done, 1)
                    if m == 1 and not last_:
                        token_transposes(e + 1, 1 - par, (2, 3))

            token_transposes(0, 0, range(4))
            experts_loop(pe, expert)
            meet(pe)


def constants():
    c = np.zeros((128, C_ALL), np.float32)
    p = np.arange(128)
    c[:, C_ID:C_ID + 128] = np.eye(128)
    c[:, C_ONES:C_ONES + 128] = p[:, None] // 8 == p[None] // 8
    c[:, C_LOW:C_LOW + 128] = (p[:, None] // 8 == p[None] // 8) & (p[:, None] < p[None])
    pos = np.arange(S)
    for qt in range(2):
        q = qt * HT + np.arange(HT)
        decay = np.exp(-0.01 * np.abs(q[:, None] - pos[None])) / 16 / WSCALE ** 2
        c[:HT, C_DECAY + qt * S:C_DECAY + (qt + 1) * S] = decay
    c[:, C_MASK] = -(p // 16 % 2)
    c[:, C_TOK:C_TOK + 64] = (np.arange(8)[None] * NJ + np.arange(NJ)[:, None]).reshape(64)
    c[:, C_ROW] = p
    c[:, C_BIT:C_BIT + 32] = 2.0 ** np.maximum(29 - np.arange(32), 0)
    c[:, C_EPS] = EPS
    return c


def kernel(x, L0_tok_conv_w, L0_tok_conv_b, L0_tok_ln_gamma, L0_tok_ln_beta, L0_attn_W_q, L0_attn_W_k, L0_attn_W_v,
           L0_attn_W_o, L0_attn_W_down_kv, L0_attn_W_up_k, L0_attn_W_up_v, L0_ffn_gate_w, L0_ffn_Wg, L0_ffn_Wu,
           L0_ffn_Wd, L0_ffn_Sg, L0_ffn_Su, L0_ffn_Sd):
    import concourse.bacc as bacc
    from concourse.bass_utils import run_bass_kernel_spmd

    a = np.asarray
    xp = np.pad(a(x), ((0, 0), (0, 1), (0, 0))).reshape(B, S, 4, 128).transpose(0, 3, 2, 1).reshape(B, 128, 4 * S)

    def twice(w):
        return np.repeat(a(w).reshape(-1, NH, 1, HD), 2, axis=2).reshape(-1, 2 * D)

    def experts(w, n):
        w = a(w)
        return w.reshape(E, w.shape[1], n, 128).transpose(0, 3, 2, 1).reshape(E, 128, n * w.shape[1])

    data = {
        "x_t": xp, "conv_w": a(L0_tok_conv_w).transpose(2, 1, 0).reshape(2 * D, D), "conv_b": L0_tok_conv_b,
        "gamma": L0_tok_ln_gamma, "beta": L0_tok_ln_beta, "wq": twice(L0_attn_W_q), "wk_t": a(L0_attn_W_k).T,
        "wv_t": a(L0_attn_W_v).T, "wo": twice(a(L0_attn_W_o).T).T, "w_down": L0_attn_W_down_kv, "w_up_k": twice(L0_attn_W_up_k),
        "w_up_v": L0_attn_W_up_v, "gate": a(L0_ffn_gate_w).T, "s_g": a(L0_ffn_Sg).T, "s_u": a(L0_ffn_Su).T,
        "s_d": a(L0_ffn_Sd).T, "e_g": experts(L0_ffn_Wg, 2), "e_u": experts(L0_ffn_Wu, 2),
        "e_d": experts(L0_ffn_Wd, 8), "const": constants(),
    }
    nc = bacc.Bacc("TRN2", target_bir_lowering=False, num_devices=1)
    data = {k: np.ascontiguousarray(a(v)) for k, v in data.items()}
    args = {k: nc.dram_tensor(k, v.shape, mybir.dt.from_np(v.dtype), kind="ExternalInput").ap() for k, v in data.items()}
    out = nc.dram_tensor("out", (T, D), F32, kind="ExternalOutput").ap()
    build(nc, **args, out=out)
    r = run_bass_kernel_spmd(nc, [data], core_ids=[0])
    return r.results[0]["out"].reshape(B, S, D)
```
